# Optimizing a Trainium2 kernel written in Bass

```python
import numpy as np
import jax
import jax.numpy as jnp

def _softmax(x, axis=-1):
    return jax.nn.softmax(x, axis=axis)

def _gelu(x):
    return jax.nn.gelu(x, approximate=True)

def _silu(x):
    return jax.nn.silu(x)

def _sigmoid(x):
    return jax.nn.sigmoid(x)

def _layernorm(x, axis=-1, eps=1e-05):
    m = jnp.mean(x, axis=axis, keepdims=True)
    v = jnp.var(x, axis=axis, keepdims=True)
    return (x - m) / jnp.sqrt(v + eps)

def _scatter_add(tgt, idx, src, axis=0):
    return tgt.at[idx].add(src)

def _segment_sum(src, seg, n):
    return jax.ops.segment_sum(src, seg, n)
kernel_name = 'mk_gnn_ffn_d1_gnn_r8_c2fb29'

def setup_inputs(seed: int=0):
    np.random.seed(seed)
    _w = jnp.asarray

    def _rec_inputs():
        import jax
        import jax.numpy as jnp
        _gk = jax.random.key(seed)
        x = -0.0002117 + 1 * jax.random.normal(jax.random.fold_in(_gk, 1), (6250, 256), jnp.float32)
        src = jax.random.randint(jax.random.fold_in(_gk, 2), (100000,), 0, 6250, jnp.int32)
        dst = jax.random.randint(jax.random.fold_in(_gk, 3), (100000,), 0, 6250, jnp.int32)
        _o = jnp.argsort(dst, stable=True)
        src = src[_o]
        dst = dst[_o]
        node_vec = -0.00472126 + 0.997171 * jax.random.normal(jax.random.fold_in(_gk, 12), (6250,), jnp.float32)
        return (x, src, dst, node_vec)
    x, src, dst, node_vec = _rec_inputs()

    def _L0_gnn_setup():
        import jax, jax.numpy as jnp
        import numpy as np
        HIDDEN = 256
        H4 = HIDDEN // 4
        N_NODES = 12500
        N_EDGES = 400000
        key = jax.random.key(seed)
        ks = jax.random.split(key, 16)
        inp = {'x': jax.random.normal(ks[0], (N_NODES, HIDDEN), dtype=jnp.float32), 'edge_index': jax.random.randint(ks[1], (2, N_EDGES), 0, N_NODES, dtype=jnp.int64), 'noise': jax.random.normal(ks[2], (N_NODES,), dtype=jnp.float32)}
        s = 1.0
        inp['W_deg'] = jax.random.normal(ks[3], (H4,), dtype=jnp.float32) * s
        inp['b_deg'] = jax.random.normal(ks[4], (H4,), dtype=jnp.float32) * s
        inp['W_bet'] = jax.random.normal(ks[5], (H4,), dtype=jnp.float32) * s
        inp['b_bet'] = jax.random.normal(ks[6], (H4,), dtype=jnp.float32) * s
        inp['W_clo'] = jax.random.normal(ks[7], (H4,), dtype=jnp.float32) * s
        inp['b_clo'] = jax.random.normal(ks[8], (H4,), dtype=jnp.float32) * s
        inp['W_eig'] = jax.random.normal(ks[9], (H4,), dtype=jnp.float32) * s
        inp['b_eig'] = jax.random.normal(ks[10], (H4,), dtype=jnp.float32) * s
        w = 1.0 / np.sqrt(HIDDEN)
        inp['W1'] = jax.random.normal(ks[11], (HIDDEN, HIDDEN), dtype=jnp.float32) * w
        inp['b1'] = jax.random.normal(ks[12], (HIDDEN,), dtype=jnp.float32) * w
        inp['W2'] = jax.random.normal(ks[13], (HIDDEN, HIDDEN), dtype=jnp.float32) * w
        inp['b2'] = jax.random.normal(ks[14], (HIDDEN,), dtype=jnp.float32) * w
        return inp
    _L0_gnn_all = _L0_gnn_setup()
    _L0_gnn_in = {k: v for k, v in _L0_gnn_all.items() if k in ('W_deg', 'b_deg', 'W_bet', 'b_bet', 'W_clo', 'b_clo', 'W_eig', 'b_eig', 'W1', 'b1', 'W2', 'b2')}
    del _L0_gnn_all

    def _L0_ffn_setup():
        import jax, jax.numpy as jnp
        import numpy as np
        E = 8
        K = 2
        D = 256
        H = 512
        DOUT = 256
        EPS = 1e-05
        key = jax.random.key(seed)
        ks = jax.random.split(key, 9)
        s = 0.02
        return {'x': jax.random.normal(ks[0], (4, 1024, D), jnp.float32), 'gamma': 1.0 + 0.05 * jax.random.normal(ks[1], (D,), jnp.float32), 'beta': 0.05 * jax.random.normal(ks[2], (D,), jnp.float32), 'Wr': 0.01 * jax.random.normal(ks[3], (D, E), jnp.float32), 'br': jnp.zeros((E,), jnp.float32), 'W1': s * jax.random.normal(ks[4], (E, D, H), jnp.float32), 'b1': s * jax.random.normal(ks[5], (E, H), jnp.float32), 'W2': s * jax.random.normal(ks[6], (E, H, DOUT), jnp.float32), 'b2': s * jax.random.normal(ks[7], (E, DOUT), jnp.float32)}
    _L0_ffn_all = _L0_ffn_setup()
    _L0_ffn_in = {k: v for k, v in _L0_ffn_all.items() if k in ('gamma', 'beta', 'Wr', 'br', 'W1', 'b1', 'W2', 'b2')}
    del _L0_ffn_all
    return {'x': x, 'src': src, 'dst': dst, 'node_vec': node_vec, 'L0_gnn_W_deg': _L0_gnn_in['W_deg'], 'L0_gnn_b_deg': _L0_gnn_in['b_deg'], 'L0_gnn_W_bet': _L0_gnn_in['W_bet'], 'L0_gnn_b_bet': _L0_gnn_in['b_bet'], 'L0_gnn_W_clo': _L0_gnn_in['W_clo'], 'L0_gnn_b_clo': _L0_gnn_in['b_clo'], 'L0_gnn_W_eig': _L0_gnn_in['W_eig'], 'L0_gnn_b_eig': _L0_gnn_in['b_eig'], 'L0_gnn_W1': _L0_gnn_in['W1'], 'L0_gnn_b1': _L0_gnn_in['b1'], 'L0_gnn_W2': _L0_gnn_in['W2'], 'L0_gnn_b2': _L0_gnn_in['b2'], 'L0_ffn_gamma': _L0_ffn_in['gamma'], 'L0_ffn_beta': _L0_ffn_in['beta'], 'L0_ffn_Wr': _L0_ffn_in['Wr'], 'L0_ffn_br': _L0_ffn_in['br'], 'L0_ffn_W1': _L0_ffn_in['W1'], 'L0_ffn_b1': _L0_ffn_in['b1'], 'L0_ffn_W2': _L0_ffn_in['W2'], 'L0_ffn_b2': _L0_ffn_in['b2']}

def reference(x, src, dst, node_vec, L0_gnn_W_deg, L0_gnn_b_deg, L0_gnn_W_bet, L0_gnn_b_bet, L0_gnn_W_clo, L0_gnn_b_clo, L0_gnn_W_eig, L0_gnn_b_eig, L0_gnn_W1, L0_gnn_b1, L0_gnn_W2, L0_gnn_b2, L0_ffn_gamma, L0_ffn_beta, L0_ffn_Wr, L0_ffn_br, L0_ffn_W1, L0_ffn_b1, L0_ffn_W2, L0_ffn_b2):
    import jax
    import jax.numpy as jnp

    def _L0_gnn_ref(x, edge_index, noise, W_deg, b_deg, W_bet, b_bet, W_clo, b_clo, W_eig, b_eig, W1, b1, W2, b2):
        import jax, jax.numpy as jnp
        import numpy as np
        HIDDEN = 256
        H4 = HIDDEN // 4
        N_NODES = 12500
        N_EDGES = 400000
        num_nodes = x.shape[0]
        col = edge_index[1]
        deg = jnp.zeros((num_nodes,), dtype=jnp.float32).at[col].add(1.0)
        degree_cent = deg / (num_nodes - 1)
        betweenness_cent = degree_cent * noise * 0.1 + degree_cent
        closeness_cent = 1.0 / (degree_cent + 1e-08)
        eigenvector_cent = jnp.sqrt(degree_cent)
        f_deg = degree_cent[:, None] * W_deg[None, :] + b_deg
        f_bet = betweenness_cent[:, None] * W_bet[None, :] + b_bet
        f_clo = closeness_cent[:, None] * W_clo[None, :] + b_clo
        f_eig = eigenvector_cent[:, None] * W_eig[None, :] + b_eig
        feats = jnp.concatenate([f_deg, f_bet, f_clo, f_eig], axis=-1)
        h = jax.nn.relu(feats @ W1 + b1)
        out = h @ W2 + b2
        return out

    def _L0_ffn_ref(x, gamma, beta, Wr, br, W1, b1, W2, b2):
        import jax, jax.numpy as jnp
        import numpy as np
        E = 8
        K = 2
        D = 256
        H = 512
        DOUT = 256
        EPS = 1e-05
        mu = jnp.mean(x, axis=-1, keepdims=True)
        var = jnp.mean(jnp.square(x - mu), axis=-1, keepdims=True)
        xn = (x - mu) * jax.lax.rsqrt(var + EPS) * gamma + beta
        logits = jnp.einsum('bsd,de->bse', xn, Wr) + br
        top_vals, top_idx = jax.lax.top_k(logits, K)
        w = jax.nn.softmax(top_vals, axis=-1)
        w_full = jnp.einsum('bsk,bske->bse', w, jax.nn.one_hot(top_idx, E, dtype=w.dtype))
        y = jnp.zeros(x.shape[:-1] + (DOUT,), x.dtype)
        for e in range(E):
            h = jax.nn.gelu(jnp.einsum('bsd,dh->bsh', xn, W1[e]) + b1[e], approximate=False)
            y_e = jnp.einsum('bsh,hd->bsd', h, W2[e]) + b2[e]
            y = y + y_e * w_full[..., e, None]
        return y
    edge_index = jnp.stack([src, dst])
    x = x + _L0_gnn_ref(_layernorm(x, axis=-1), edge_index, node_vec, L0_gnn_W_deg, L0_gnn_b_deg, L0_gnn_W_bet, L0_gnn_b_bet, L0_gnn_W_clo, L0_gnn_b_clo, L0_gnn_W_eig, L0_gnn_b_eig, L0_gnn_W1, L0_gnn_b1, L0_gnn_W2, L0_gnn_b2)
    x = x + _L0_ffn_ref(_layernorm(x, axis=-1)[None], L0_ffn_gamma, L0_ffn_beta, L0_ffn_Wr, L0_ffn_br, L0_ffn_W1, L0_ffn_b1, L0_ffn_W2, L0_ffn_b2)[0]
    return x

_drawn_inputs = setup_inputs


def setup_inputs(seed=0):
    import zlib

    import numpy as np

    out = dict(_drawn_inputs(seed))
    spreads = {'L0_ffn_br': (0.0, 2.0)}
    factors = {'x': 8.0,
     'node_vec': 200.0,
     'L0_gnn_W_deg': 200.0,
     'L0_gnn_b_deg': 8.0,
     'L0_gnn_W_bet': 200.0,
     'L0_gnn_b_bet': 8.0,
     'L0_gnn_b_clo': 23.654,
     'L0_gnn_W_eig': 200.0,
     'L0_gnn_b_eig': 8.0,
     'L0_gnn_b1': 175.947,
     'L0_gnn_b2': 64.0,
     'L0_ffn_gamma': 27.023,
     'L0_ffn_beta': 28.311,
     'L0_ffn_Wr': 8.0,
     'L0_ffn_W1': 8.0,
     'L0_ffn_b1': 200.0,
     'L0_ffn_W2': 8.0,
     'L0_ffn_b2': 200.0}
    for name, (base, spread) in spreads.items():
        noise = np.random.default_rng([zlib.crc32(name.encode()), seed]).standard_normal(out[name].shape)
        drawn = base * np.exp(spread * noise) if base else spread * noise
        out[name] = jnp.asarray(drawn.astype(out[name].dtype))
    for name, factor in factors.items():
        out[name] = (out[name] * factor).astype(out[name].dtype)
    return out
```

```python
from contextlib import ExitStack

import concourse.bass as bass
from concourse import mybir

ALU = mybir.AluOpType
ACT = mybir.ActivationFunctionType
AX_X = mybir.AxisListType.X
F32 = mybir.dt.float32
F32R = mybir.dt.float32r
BF16 = mybir.dt.bfloat16
I32 = mybir.dt.int32
U32 = mybir.dt.uint32

P = 128
LN_EPS = 1e-5

LO = 64
OH_TILES = 16

GROUP = 7
RINGS = 3


GNN_LOADS = 15

SIGNALS = """
    dst_in small_in gnn_in stage_a stage_b zeroed numbers consts prep_done spare_sent bias_moved
    beta_ready beta_now beta_w1 beta_b1 bias_ps mix_ps mix_copied mix_ready wrg_ready
    w1_high w2_high w1_low w2_low onehot onehot_used degree sqrt_in sqrt_out feats_ready feat_kept feat_zeroed
    pool_step act_step dve_step
    hid_ps hid_ready gnn_ps x1_ready x1_kept stats_ready var_ready std_ready norm_ready
    u_ready ut_ps ut_ready logit_ps logits_read mask_ready pos_ps dest_ready fill_ready table_ready
    pads_sent gap_ready exp_ready
    xt_ps xth_ready xt_ready yoff_ready yrow_ready h_ps h_ready ht_ps hth_ready htl_ready y_ps y_ready
    x1_back half_summed summed stored carried
""".split()


def gnn_ffn_kernel(nc, x, dst, node_vec, g_wdeg, g_bdeg, g_wbet, g_bbet, g_wclo, g_bclo, g_weig, g_beig,
                   g_w1, g_b1, g_w2, g_b2, gamma, beta, wr, br, w1, b1, w2, b2, out):
    N, D = x.shape
    E, _, H = w1.shape
    n_edges = dst.shape[0]
    KD, KH = D // P, H // P
    TILES = -(-N // P)
    TAIL = N - (TILES - 1) * P
    GROUPS = TILES // GROUP
    assert GROUPS * GROUP == TILES and GROUPS == 2 * RINGS + 1 and D == 256 and H == 512 and E == 8
    NPAD = TILES * P
    HI = NPAD // LO
    EP = 125
    ECOLS = n_edges // EP
    CHUNKS = ECOLS // OH_TILES
    assert EP * ECOLS == n_edges and CHUNKS * OH_TILES == ECOLS and CHUNKS % 2 == 0
    REGION = NPAD + P
    ROW = D + 2
    SLOT_TILES = (2 * N + E * (P - 1)) // P
    SPARE = SLOT_TILES - 2 * N // P + 1
    SPARE_AT = E * REGION
    assert SLOT_TILES % 4 == 1

    with ExitStack() as ctx:
        def sb(name, shape, dt):
            return ctx.enter_context(nc.sbuf_tensor(name, shape, dt))

        def sem(name):
            return ctx.enter_context(nc.semaphore(name))

        ctx.enter_context(nc.allow_low_precision(reason="sums of row numbers are exact integers in float32"))
        ctx.enter_context(nc.allow_non_contiguous_dma(reason="a few short vectors are laid over partitions"))

        feat_dram = nc.dram_tensor("feat_dram", (5, NPAD), F32).ap()
        x1_dram = nc.dram_tensor("x1_dram", (NPAD, D), F32).ap()
        routed = nc.dram_tensor("routed", (SPARE_AT + SPARE * P, ROW), F32).ap()
        y_dram = nc.dram_tensor("y_dram", (2 * N + (E + SPARE) * P, D), F32).ap()

        w1h = sb("w1h", [P, E * KD * H], F32R)
        w1l = sb("w1l", [P, E * KD * H], F32R)
        w2h = sb("w2h", [P, E * KH * D], F32R)
        w2l = sb("w2l", [P, E * KH * D], F32R)
        sel = sb("sel", [P, E, P], BF16)
        b1s = sb("b1s", [P, H], BF16)
        b2s = sb("b2s", [P, D], BF16)
        ident = sb("ident", [P, P], F32)
        below = sb("below", [P, P], BF16)
        ones = sb("ones", [P, P], BF16)
        wr_g = sb("wr_g", [P, KD, E], F32)
        br_bc = sb("br_bc", [P, E], F32)
        rev = sb("rev", [P, E], F32)
        node_id = sb("node_id", [P, TILES], F32)
        gap = sb("gap", [P, TILES], F32)
        wa = sb("wa", [P, TILES], F32)
        wb = sb("wb", [P, TILES], F32)
        fill = sb("fill", [P, E], F32)
        slot_e = sb("slot_e", [P, SLOT_TILES], F32)
        slot_ei = sb("slot_ei", [P, SLOT_TILES], I32)
        slot_row = sb("slot_row", [P, SLOT_TILES], I32)

        xg = sb("xg", [P, 2, ROW], F32)
        xth = sb("xth", [P, 2, KD, P], F32R)
        xtl = sb("xtl", [P, 2, KD, P], F32R)
        hbuf = sb("hbuf", [P, 2, H], F32)
        hth = sb("hth", [P, 2, KH, P], F32R)
        htl = sb("htl", [P, 2, KH, P], F32R)
        ybuf = sb("ybuf", [P, 2, D], F32)
        y_row = sb("y_row", [P, 4, 1], U32)
        y_off = sb("y_off", [P, 2, 1], F32)
        stage_w1 = hbuf[:, :, :].rearrange("p b h -> p (b h)").rearrange("p (k h) -> p k h", k=KD)

        gb = sb("gb", [P, 2, KD], F32)
        stats = sb("stats", [P, GROUP, 6], F32)
        mv = sb("mv", [P, GROUP, 2], F32)
        rt = sb("rt", [P, 6, GROUP], F32)
        rstd = sb("rstd", [P, RINGS, GROUP], F32)
        nmean = sb("nmean", [P, RINGS, GROUP], F32)
        lg = sb("lg", [P, GROUP, E], F32)
        lg2 = sb("lg2", [P, GROUP, E], F32)
        eqm = sb("eqm", [P, GROUP, E], F32)
        oh1 = sb("oh1", [P, GROUP, E], F32)
        oh2 = sb("oh2", [P, GROUP, E], F32)
        both = sb("both", [P, 2 * GROUP + 1, E], BF16)
        posE = sb("posE", [P, GROUP, E], F32)
        m1 = sb("m1", [P, GROUP], F32)
        m2 = sb("m2", [P, GROUP], F32)
        r1 = sb("r1", [P, GROUP], F32)
        r2 = sb("r2", [P, GROUP], F32)
        valid = sb("valid", [P, 1], F32)
        dest = sb("dest", [P, RINGS, 2, GROUP], U32)
        pad_dest = sb("pad_dest", [P, E], U32)
        cnt_i = sb("cnt_i", [P, E], I32)
        ntile_i = sb("ntile_i", [P, E], I32)
        ntile = sb("ntile", [P, E], F32)
        cum = sb("cum", [P, 2, 4 + E], F32)
        jump = sb("jump", [P, E], F32)
        spare_ids = sb("spare_ids", [P, SPARE, 2], F32)

        arena = sb("arena", [P, TILES * D], F32)
        used = [0]

        def view(words, at=None):
            at = used[0] if at is None else at
            used[0] = max(used[0], at + words)
            assert used[0] <= TILES * D
            return arena[:, at:at + words]

        RW = GROUP * ROW
        ring = [view(RW).rearrange("p (j r) -> p j r", r=ROW) for _ in range(2)]
        top = used[0]
        oh_hi = view(2 * HI * OH_TILES // 2).bitcast(BF16).rearrange("p (b j t) -> p b j t", b=2, t=OH_TILES)
        oh_lo = view(2 * LO * OH_TILES // 2).bitcast(BF16).rearrange("p (b j t) -> p b j t", b=2, t=OH_TILES)
        num_hi = view(HI * OH_TILES // 2).bitcast(BF16).rearrange("p (j t) -> p j t", t=OH_TILES)
        num_lo = view(LO * OH_TILES // 2).bitcast(BF16).rearrange("p (j t) -> p j t", t=OH_TILES)
        dst_hi = view(ECOLS // 2).bitcast(BF16)
        dst_lo = view(ECOLS // 2).bitcast(BF16)
        at_dst = used[0]
        dst_i = view(ECOLS).bitcast(I32)
        hi_i = view(ECOLS).bitcast(I32)
        lo_i = view(ECOLS).bitcast(I32)
        w2g = view(KD * D).rearrange("p (k d) -> p k d", k=KD)
        w1g = view(KD * D).rearrange("p (k d) -> p k d", k=KD)
        mix = view(D)
        b2g = view(D // 2).bitcast(BF16)
        ring.append(view(RW, top).rearrange("p (j r) -> p j r", r=ROW))
        feat = view(2 * GROUP * P, top + RW).rearrange("p (b n) -> p b n", b=2)
        fw = view(12 * LO, top + RW + 2 * GROUP * P)[0:HI, :].rearrange("p (f l) -> p f l", f=12)
        assert top + RW + 2 * GROUP * P + 12 * LO <= at_dst
        u_t = view(2 * D, at_dst).rearrange("p (b k n) -> p b k n", b=2, k=KD)
        g_t = view(2 * D, at_dst + 2 * D).rearrange("p (b k n) -> p b k n", b=2, k=KD)
        pad_rows = view(E * ROW, top + RW).rearrange("p (e r) -> p e r", e=E)
        cmp_a = view(SLOT_TILES * E, at_dst).rearrange("p (s e) -> p s e", e=E)
        cmp_b = view(SLOT_TILES * E, at_dst + SLOT_TILES * E).rearrange("p (s e) -> p s e", e=E)
        slot_f = view(SLOT_TILES, at_dst + 2 * SLOT_TILES * E)
        stage_w2 = view(KH * D, 0).rearrange("p (k d) -> p k d", k=KH)
        bias_f = view(H, RW)[0:E, :]
        bias_p = view(3 * H // 2, RW + H).bitcast(BF16).rearrange("p (q n) -> p q n", q=3)[0:E, :, :]
        beta_e = view(KD * E * E, RW + H + 3 * H // 2).rearrange("p (k a) -> p k a", k=KD)
        at = RW + H + 3 * H // 2 + KD * E * E
        noise = view(LO, at)[0:HI, :]
        wr_raw = view(KD * E, at + LO).rearrange("p (k e) -> p k e", k=KD)
        vec_w = view(KD * 5, at + LO + KD * E).rearrange("p (k q) -> p k q", k=KD)
        beta_bc = view(KD * P, at + LO + KD * E + KD * 5).rearrange("p (k m) -> p k m", k=KD)
        mix_bias = xg[0:5, 0, 0:D]
        x1_back = arena[:, :].rearrange("p (t d) -> p t d", d=D)
        zeros = ybuf[:, 0, :]
        beta_b1 = ybuf[:, :, :].rearrange("p b d -> p (b d)")[0:E, :]
        beta_now = sb("beta_now", [P, KD, E], F32)
        fence = sb("fence", [P, 1], F32)
        fence_end = stats[:, 0, 0:1]
        regions = sb("regions", [P, E], F32)
        br_raw = sb("br_raw", [P, E], F32)[:, :]
        slot_no = sb("slot_no", [P, SLOT_TILES], F32)

        bank = [ctx.enter_context(nc.psum_tensor(f"bank{i}", [P, 512], F32)) for i in range(8)]

        S = {}
        for name in SIGNALS:
            S[name] = sem("s_" + name)
        x_in = [sem(f"s_x_in{r}") for r in range(RINGS)]
        feat_in = [sem(f"s_feat_in{r}") for r in range(2)]
        sent = [sem(f"s_sent{r}") for r in range(RINGS)]
        xg_in = [sem(f"s_xg_in{r}") for r in range(2)]
        y_sent = [sem(f"s_y_sent{r}") for r in range(2)]
        y_back = [sem(f"s_y_back{g}") for g in range(GROUPS)]

        block = ctx.enter_context(nc.Block())

        w1_dram = w1.rearrange("e (k p) h -> e p k h", p=P)
        w2_dram = w2.rearrange("e (k p) d -> e p k d", p=P)

        def group_parts(dram, g):
            first = g * GROUP
            whole = GROUP if first + GROUP < TILES or dram.shape[0] == NPAD else GROUP - 1
            parts = [(P, slice(0, whole), dram[first * P:(first + whole) * P, :].rearrange("(j p) d -> p j d", p=P))]
            if whole < GROUP:
                parts.append((TAIL, whole, dram[(first + whole) * P:N, :]))
            return parts

        def ring_step(j):
            return {0: 1, 1: 3}.get(j, 2)

        def y_parts(g):
            home = (w1h, w1l, w2h, w2l)[g // 2][:, :].bitcast(F32)
            at = (g % 2) * 2 * GROUP * D
            return [home[:, at + k * GROUP * D:at + (k + 1) * GROUP * D].rearrange("p (j d) -> p j d", d=D)
                    for k in range(2)]

        @block.sync
        def _(sp):
            sp.dma_start(dst_i[0:EP, :], dst.rearrange("(p c) -> p c", c=ECOLS)).then_inc(S["dst_in"], 16)
            sp.dma_start(gb[:, 0, :], gamma.rearrange("(k p) -> p k", p=P)).then_inc(S["small_in"], 16)
            sp.dma_start(gb[:, 1, :], beta.rearrange("(k p) -> p k", p=P)).then_inc(S["small_in"], 16)
            sp.dma_start(stage_w1, w1_dram[0]).then_inc(S["stage_a"], 16)
            sp.dma_start(stage_w2, w2_dram[0]).then_inc(S["stage_b"], 16)
            sp.dma_start(wr_raw, wr.rearrange("(k p) e -> p k e", p=P)).then_inc(S["gnn_in"], 16)
            sp.dma_start(w1g, g_w1.rearrange("(k p) h -> p k h", p=P)).then_inc(S["gnn_in"], 16)
            sp.dma_start(w2g, g_w2.rearrange("(k p) h -> p k h", p=P)).then_inc(S["gnn_in"], 16)
            sp.wait_ge(S["zeroed"], 1)
            for q, (wv, bv) in enumerate([(g_wdeg, g_bdeg), (g_wbet, g_bbet), (g_wclo, g_bclo), (g_weig, g_beig)]):
                rows = slice(64 * (q % 2), 64 * (q % 2) + 64)
                sp.dma_start(vec_w[rows, q // 2, q:q + 1], wv.rearrange("(p a) -> p a", a=1)).then_inc(S["gnn_in"], 16)
                sp.dma_start(vec_w[rows, q // 2, 4:5], bv.rearrange("(p a) -> p a", a=1)).then_inc(S["gnn_in"], 16)
            sp.dma_start(mix_bias[4:5, :], g_b1.rearrange("(a d) -> a d", a=1)).then_inc(S["gnn_in"], 16)
            sp.dma_start(noise[0:HI - 1, :], node_vec[0:(HI - 1) * LO].rearrange("(h l) -> h l", l=LO)).then_inc(S["gnn_in"], 16)
            sp.dma_start(noise[HI - 1:HI, 0:N - (HI - 1) * LO],
                         node_vec[(HI - 1) * LO:N].rearrange("(a l) -> a l", a=1)).then_inc(S["gnn_in"], 16)
            sp.dma_start(br_raw, br.rearrange("(a e) -> a e", a=1).to_broadcast([P, E])).then_inc(S["gnn_in"], 16)
            with sp.Fori(1, E) as e:
                sp.wait_ge(S["w1_low"], e)
                sp.dma_start(stage_w1, w1_dram[bass.ds(e, 1)].rearrange("a p k h -> p (a k) h")).then_inc(S["stage_a"], 16)
                sp.wait_ge(S["w2_low"], e)
                sp.dma_start(stage_w2, w2_dram[bass.ds(e, 1)].rearrange("a p k d -> p (a k) d")).then_inc(S["stage_b"], 16)

            def load_x(g):
                for rows, j, part in group_parts(x, g):
                    sp.dma_start(ring[g % RINGS][0:rows, j, 0:D], part).then_inc(x_in[g % RINGS], 16)

            def load_features(g):
                sp.dma_start(feat[0:5, g % 2, :], feat_dram[:, g * GROUP * P:(g + 1) * GROUP * P]).then_inc(feat_in[g % 2], 16)

            sp.wait_ge(S["w2_low"], E)
            load_x(0)
            sp.wait_ge(S["prep_done"], 1)
            sp.wait_ge(S["feats_ready"], 1)
            sp.dma_start(feat_dram.rearrange("f (h l) -> h f l", l=LO), fw[:, 0:5, :]).then_inc(S["feat_kept"], 16)
            load_x(1)
            sp.wait_ge(S["feat_kept"], 16)
            sp.wait_ge(S["feat_zeroed"], 1)
            load_features(0)
            load_features(1)
            load_x(2)
            for g in range(GROUPS):
                sp.wait_ge(S["x1_ready"], GROUP * (g + 1))
                sp.dma_start(x1_dram[g * GROUP * P:(g + 1) * GROUP * P, :].rearrange("(j p) d -> p j d", p=P),
                             ring[g % RINGS][:, :, 0:D]).then_inc(S["x1_kept"], 16)
                if g + 2 < GROUPS:
                    sp.wait_ge(S["hid_ps"], GROUP * (g + 1))
                    load_features(g + 2)
                if g >= 1 and g + 2 < GROUPS:
                    sp.wait_ge(sent[(g - 1) % RINGS], 32 * GROUP * ((g - 1) // RINGS + 1))
                    load_x(g + 2)

            def load_slot(s, b):
                row = sp.value_load(slot_row[0:1, bass.ds(s, 1)], min_val=0, max_val=SPARE_AT + (SPARE - 1) * P)
                sp.dma_start(xg[:, b, :], routed[bass.ds(row, P), :]).then_inc(xg_in[b], 16)

            sp.wait_ge(S["table_ready"], 1)
            for r in range(RINGS):
                sp.wait_ge(sent[r], 32 * GROUP * len(range(r, GROUPS, RINGS)))
            sp.wait_ge(S["pads_sent"], 16 * E)
            sp.wait_ge(S["spare_sent"], 32)
            load_slot(0, 0)
            load_slot(1, 1)
            sp.wait_ge(S["x1_kept"], 16 * GROUPS)
            sp.dma_start(x1_back, x1_dram.rearrange("(t p) d -> p t d", p=P)).then_inc(S["x1_back"], 16)
            with sp.Fori(1, SLOT_TILES // 2) as i:
                for b in range(2):
                    sp.wait_ge(S["yrow_ready"], 2 * i + b - 1)
                    sp.wait_ge(S["xt_ps"], 2 * i + b - 1)
                    load_slot(2 * i + b, b)
            sp.wait_ge(S["yrow_ready"], SLOT_TILES - 2)
            sp.wait_ge(S["xt_ps"], SLOT_TILES - 2)
            load_slot(SLOT_TILES - 1, 0)

            sp.wait_ge(y_sent[0], 16 * (SLOT_TILES // 2 + 1))
            sp.wait_ge(y_sent[1], 16 * (SLOT_TILES // 2))
            for g in range(GROUPS):
                for k in range(2):
                    for rows, j, part in group_parts(y_dram[k * N:(k + 1) * N, :], g):
                        sp.dma_start(y_parts(g)[k][0:rows, j, :], part).then_inc(y_back[g], 16)
            for g in range(GROUPS):
                sp.wait_ge(S["summed"], GROUP * (g + 1))
                for rows, j, part in group_parts(out, g):
                    first = g * GROUP
                    src = x1_back[0:rows, first + j.start:first + j.stop, :] if isinstance(j, slice) else x1_back[0:rows, first + j, :]
                    sp.dma_start(part, src).then_inc(S["stored"], 16)
            sp.wait_ge(S["stored"], 16 * (GROUPS + 1))

        @block.gpsimd
        def _(pool):
            steps = [0]

            def then(ins):
                steps[0] += 1
                ins.then_inc(S["pool_step"], 1)
                pool.wait_ge(S["pool_step"], steps[0])

            for q, (t, n) in enumerate([(num_hi, HI), (num_lo, LO)]):
                pool.iota(t, pattern=[[1, n], [0, OH_TILES]], base=0, channel_multiplier=0,
                          allow_small_or_imprecise_dtypes=True).then_inc(S["numbers"], 1)
            then(pool.memset(vec_w, 0.0))
            then(pool.memset(mix_bias, 0.0))
            then(pool.memset(noise, 0.0))
            then(pool.memset(zeros[:], 0.0))
            pool.memset(fence[:], 0.0).then_inc(S["zeroed"], 1)
            then(pool.iota(spare_ids[:, :, 0], pattern=[[P, SPARE]], base=N + E * P, channel_multiplier=1,
                           allow_small_or_imprecise_dtypes=True))
            then(pool.memset(spare_ids[:, :, 1], -1.0))
            spare = routed[SPARE_AT:SPARE_AT + SPARE * P, :].rearrange("(j p) r -> p j r", p=P)
            pool.dma_start(spare[:, :, 0:D], zeros[:, :].unsqueeze(1).to_broadcast([P, SPARE, D])).then_inc(S["spare_sent"], 16)
            pool.dma_start(spare[:, :, D:ROW], spare_ids[:]).then_inc(S["spare_sent"], 16)
            then(pool.memset(beta_e, 0.0))
            pool.wait_ge(S["small_in"], 32)
            for k in range(KD):
                pool.tensor_copy(beta_e[:, k, 0:E * E:E + 1], gb[:, 1, k:k + 1].to_broadcast([P, E])).then_inc(S["beta_ready"], 1)
                pool.tensor_copy(beta_bc[:, k, :], gb[:, 1, k:k + 1].to_broadcast([P, P])).then_inc(S["beta_ready"], 1)
            then(pool.memset(ident[:], 0.0))
            then(pool.affine_select(out=ident[:], in_=ident[:], compare_op=ALU.not_equal, fill=1.0, base=0,
                                    pattern=[[-1, P]], channel_multiplier=1))
            then(pool.memset(ones[:], 1.0))
            then(pool.affine_select(out=below[:], in_=ones[:], compare_op=ALU.is_gt, fill=0.0, base=0,
                                    pattern=[[1, P]], channel_multiplier=-1))
            then(pool.memset(sel[:], 0.0))
            for part in range(4):
                then(pool.affine_select(out=sel[:], in_=sel[:], compare_op=ALU.not_equal, fill=1.0, base=-32 * part,
                                        pattern=[[-1, E], [0, P]], channel_multiplier=1))
            for t, step, n, base, per_row in ((rev, -1, E, E, 0), (fill, REGION, E, 0, 0), (regions, REGION, E, 0, 0),
                                              (node_id, P, TILES, 0, 1), (slot_no, 1, SLOT_TILES, 0, 0)):
                then(pool.iota(t[:], pattern=[[step, n]], base=base, channel_multiplier=per_row,
                               allow_small_or_imprecise_dtypes=True))
            then(pool.memset(both[:], 0.0))
            then(pool.memset(b1s[:], 0.0))
            then(pool.memset(b2s[:], 0.0))
            then(pool.memset(b2g, 0.0))
            then(pool.memset(mix, 0.0))
            pool.memset(fence[:], 0.0).then_inc(S["consts"], 1)

            moved = [0]

            def split_bias(rows, n, home):
                f = bias_f[0:rows, 0:n]
                then(pool.tensor_copy(bias_p[0:rows, 0, 0:n], f))
                then(pool.tensor_tensor(f, f, bias_p[0:rows, 0, 0:n], ALU.subtract))
                then(pool.tensor_copy(bias_p[0:rows, 1, 0:n], f))
                then(pool.tensor_tensor(f, f, bias_p[0:rows, 1, 0:n], ALU.subtract))
                then(pool.tensor_copy(bias_p[0:rows, 2, 0:n], f))
                for q in range(3):
                    pool.dma_start(home[32 * q:32 * q + rows, 0:n], bias_p[0:rows, q, 0:n]).then_inc(S["bias_moved"], 16)
                    moved[0] += 16
                pool.wait_ge(S["bias_moved"], moved[0])

            for rows, dram, home in ((1, g_b2.rearrange("(a d) -> a d", a=1), b2g), (E, b2, b2s)):
                pool.dma_start(bias_f[0:rows, 0:D], dram).then_inc(S["bias_moved"], 16)
                moved[0] += 16
                pool.wait_ge(S["bias_moved"], moved[0])
                split_bias(rows, D, home)

            with pool.Fori(0, E) as e:
                pool.wait_ge(S["w1_high"], e + 1)
                at = bass.ds(e * (KD * H), KD * H)
                pool.tensor_tensor(w1l[:, at], stage_w1.rearrange("p k h -> p (k h)"), w1h[:, at].bitcast(F32),
                                   ALU.subtract).then_inc(S["w1_low"], 1)
                pool.wait_ge(S["w2_high"], e + 1)
                pool.tensor_tensor(w2l[:, at], stage_w2.rearrange("p k d -> p (k d)"), w2h[:, at].bitcast(F32),
                                   ALU.subtract).then_inc(S["w2_low"], 1)
            pool.dma_start(bias_f[:, :], b1).then_inc(S["bias_moved"], 16)
            moved[0] += 16
            pool.wait_ge(S["bias_moved"], moved[0])
            pool.wait_ge(S["beta_b1"], 1)
            then(pool.tensor_tensor(bias_f, bias_f, beta_b1, ALU.add))
            split_bias(E, H, b1s)
            pool.wait_ge(S["mix_copied"], 2)
            pool.tensor_tensor(mix[0:5, :], mix[0:5, :], mix_bias, ALU.add).then_inc(S["mix_ready"], 1)
            then(pool.tensor_tensor(br_bc[:], br_bc[:], br_raw, ALU.add))
            then(pool.memset(fence[:], 0.0))
            pool.memset(fence_end[:], 0.0).then_inc(S["prep_done"], 1)
            pool.wait_ge(S["prep_done"], 1)
            pool.memset(fence_end[:], 0.0).then_inc(S["carried"], 1)
            pool.wait_ge(S["feats_ready"], 1)
            pool.memset(feat, 0.0).then_inc(S["feat_zeroed"], 1)

            def carry_wait(n):
                pool.wait_ge(S["carried"], n + 1)
                pool.tensor_tensor(fence[:], fence[:], fence[:], ALU.add).then_inc(S["carried"], 1)

            def scatter(g, r, last=False):
                pool.wait_ge(S["dest_ready"], g + 1)
                carry_wait(g)
                for k in range(2):
                    for j in range(GROUP):
                        rows = TAIL if last and j == GROUP - 1 else P
                        pool.indirect_dma_start(
                            out=routed[:, :], out_offset=bass.IndirectOffsetOnAxis(dest[0:rows, r, k, j:j + 1], 0),
                            in_=ring[r][0:rows, j, :], in_offset=None).then_inc(sent[r], 16)

            with pool.Fori(0, 2) as i:
                for a in range(RINGS):
                    scatter(RINGS * i + a, a)
            pool.wait_ge(S["hid_ps"], TILES)
            then(pool.memset(pad_rows, 0.0))
            then(pool.iota(pad_rows[:, :, D], pattern=[[P, E]], base=N, channel_multiplier=1,
                           allow_small_or_imprecise_dtypes=True))
            then(pool.memset(pad_rows[:, :, D + 1], -1.0))
            scatter(GROUPS - 1, (GROUPS - 1) % RINGS, last=True)
            pool.wait_ge(S["fill_ready"], 1)
            for e in range(E):
                pool.indirect_dma_start(
                    out=routed[:, :], out_offset=bass.IndirectOffsetOnAxis(pad_dest[:, e:e + 1], 0),
                    in_=pad_rows[:, e, :], in_offset=None).then_inc(S["pads_sent"], 16)

            def send_y(s, q):
                pool.wait_ge(S["yrow_ready"], s + 1)
                pool.wait_ge(S["y_ready"], s + 1)
                carry_wait(GROUPS + s)
                pool.indirect_dma_start(out=y_dram[:, :], out_offset=bass.IndirectOffsetOnAxis(y_row[:, q, :], 0),
                                        in_=ybuf[:, q % 2, :], in_offset=None).then_inc(y_sent[q % 2], 16)

            with pool.Fori(0, SLOT_TILES // 4) as i:
                for q in range(4):
                    send_y(4 * i + q, q)
            send_y(SLOT_TILES - 1, 0)

        @block.scalar
        def _(act):
            act.wait_ge(S["small_in"], 32)
            act.wait_ge(S["beta_ready"], 2 * KD)
            with act.Fori(0, E) as e:
                act.wait_ge(S["beta_w1"], e + 1)
                act.copy(beta_now[:], beta_e[:, :, bass.ds(e * E, E)]).then_inc(S["beta_now"], 1)
                act.wait_ge(S["beta_w1"], e + 2)
                for k in range(KD):
                    act.activation(stage_w1[:, k, :], stage_w1[:, k, :], ACT.Copy, scale=gb[:, 0, k:k + 1]).then_inc(S["act_step"], 1)
                act.wait_ge(S["act_step"], KD * e + KD)
                act.copy(w1h[:, bass.ds(e * (KD * H), KD * H)], stage_w1.rearrange("p k h -> p (k h)")).then_inc(S["w1_high"], 1)
                act.wait_ge(S["stage_b"], 16 * e + 16)
                act.copy(w2h[:, bass.ds(e * (KH * D), KH * D)], stage_w2.rearrange("p k d -> p (k d)")).then_inc(S["w2_high"], 1)
            act.wait_ge(S["gnn_in"], 16 * GNN_LOADS)
            for k in range(KD):
                act.activation(wr_g[:, k, :], wr_raw[:, k, :], ACT.Copy, scale=gb[:, 0, k:k + 1]).then_inc(S["wrg_ready"], 1)
            act.wait_ge(S["bias_ps"], 1)
            act.copy(beta_b1, bank[1][0:E, 0:H]).then_inc(S["beta_b1"], 1)
            act.wait_ge(S["consts"], 1)
            act.wait_ge(S["mix_ps"], 2)
            act.copy(mix[0:5, :], bank[2][0:5, 0:D]).then_inc(S["mix_copied"], 1)
            act.copy(br_bc[:], bank[3][:, 0:E]).then_inc(S["mix_copied"], 1)
            act.wait_ge(S["sqrt_in"], 1)
            act.activation(fw[:, 6, :], fw[:, 9, :], ACT.Sqrt).then_inc(S["sqrt_out"], 1)

            def normalise(t, j, r):
                act.activation(ring[r][:, j, 0:D], ring[r][:, j, 0:D], ACT.Identity,
                               bias=nmean[:, r, j:j + 1], scale=rstd[:, r, j:j + 1]).then_inc(S["u_ready"], 1)

            def relu(t, j, first=False):
                act.wait_ge(S["hid_ps"], t + 1)
                if not (first and j < 2):
                    act.wait_ge(S["gnn_ps"], t - ring_step(j) + 1)
                act.activation(g_t[:, j % 2, :, :], bank[4 + j % 2][:, 0:KD * P].rearrange("p (k n) -> p k n", k=KD),
                               ACT.Relu).then_inc(S["hid_ready"], 1)

            def keep_ut(t, j, first=False):
                act.wait_ge(S["ut_ps"], t + 1)
                if not (first and j < 2):
                    act.wait_ge(S["logit_ps"], t - ring_step(j) + 1)
                act.copy(u_t[:, j % 2, :, :], bank[2 + j % 2][:, 0:KD * P].rearrange("p (k n) -> p k n", k=KD)).then_inc(S["ut_ready"], 1)

            def root(g):
                act.wait_ge(S["var_ready"], g + 1)
                act.activation(rt[:, 1, :], rt[:, 0, :], ACT.Sqrt).then_inc(S["std_ready"], 1)

            def group(g, r, r_last, hidden=True, router=True, first=False, second=False):
                if router:
                    act.wait_ge(S["norm_ready"], g)
                    act.wait_ge(S["x1_kept"], 16 * g)
                    normalise(GROUP * (g - 1), 0, r_last)
                for j in range(GROUP):
                    if hidden:
                        relu(GROUP * g + j, j, first)
                    if router:
                        if j + 1 < GROUP:
                            normalise(GROUP * (g - 1) + j + 1, j + 1, r_last)
                        keep_ut(GROUP * (g - 1) + j, j, second)
                if hidden:
                    root(g)

            group(0, 0, None, router=False, first=True)
            group(1, 1, 0, second=True)
            group(2, 2, 1)
            group(3, 0, 2)
            with act.Fori(1, 2) as i:
                for a in range(RINGS):
                    group(RINGS * i + a + 1, (a + 1) % RINGS, a)
            group(GROUPS, None, (GROUPS - 1) % RINGS, hidden=False)
            act.wait_ge(S["gap_ready"], 1)
            act.activation(wb[:], gap[:], ACT.Exp).then_inc(S["exp_ready"], 1)

            def gelu(s, b):
                act.wait_ge(S["h_ps"], s + 1)
                act.activation(hbuf[:, b, :], bank[1 + b][:, :], ACT.Gelu).then_inc(S["h_ready"], 1)

            def high_ht(s, b, first=False):
                act.wait_ge(S["ht_ps"], s + 1)
                if not first:
                    act.wait_ge(S["y_ps"], s - 1)
                act.copy(hth[:, b, :, :], bank[3 + b][:, :].rearrange("p (k n) -> p k n", k=KH)).then_inc(S["hth_ready"], 1)

            def keep_y(s, b, sent_before):
                act.wait_ge(S["y_ps"], s + 1)
                if sent_before is not None:
                    act.wait_ge(y_sent[b], sent_before)
                act.copy(ybuf[:, b, :], bank[5 + b][:, 0:D]).then_inc(S["y_ready"], 1)

            gelu(0, 0)
            gelu(1, 1)
            high_ht(0, 0, first=True)
            gelu(2, 0)
            high_ht(1, 1, first=True)
            keep_y(0, 0, None)
            gelu(3, 1)
            high_ht(2, 0)
            keep_y(1, 1, None)
            with act.Fori(2, SLOT_TILES // 2) as i:
                for b in range(2):
                    gelu(2 * i + b, b)
                    high_ht(2 * i + b - 1, 1 - b)
                    keep_y(2 * i + b - 2, b, 16 * (i - 1))
            gelu(SLOT_TILES - 1, 0)
            high_ht(SLOT_TILES - 2, 1)
            keep_y(SLOT_TILES - 3, 0, 16 * (SLOT_TILES // 2 - 1))
            high_ht(SLOT_TILES - 1, 0)
            keep_y(SLOT_TILES - 2, 1, 16 * (SLOT_TILES // 2 - 1))
            keep_y(SLOT_TILES - 1, 0, 16 * (SLOT_TILES // 2))

        @block.vector
        def _(dve):
            steps = [0]

            def then(ins, base=None):
                steps[0] += 1
                ins.then_inc(S["dve_step"], 1)
                dve.wait_ge(S["dve_step"], steps[0] if base is None else base + steps[0])

            dve.wait_ge(S["dst_in"], 16)
            dve.tensor_scalar(hi_i[0:EP, :], dst_i[0:EP, :], 6, None, ALU.logical_shift_right).then_inc(S["dve_step"], 1)
            dve.tensor_scalar(lo_i[0:EP, :], dst_i[0:EP, :], LO - 1, None, ALU.bitwise_and).then_inc(S["dve_step"], 1)
            steps[0] += 2
            dve.wait_ge(S["dve_step"], 2)
            dve.tensor_copy(dst_hi[0:EP, :], hi_i[0:EP, :]).then_inc(S["dve_step"], 1)
            dve.tensor_copy(dst_lo[0:EP, :], lo_i[0:EP, :]).then_inc(S["dve_step"], 1)
            steps[0] += 2
            dve.wait_ge(S["dve_step"], 4)
            dve.wait_ge(S["numbers"], 2)

            def onehots(c, b):
                cols = bass.ds(c * OH_TILES, OH_TILES)
                dve.tensor_tensor(oh_hi[0:EP, b, :, :], dst_hi[0:EP, cols].unsqueeze(1).to_broadcast([EP, HI, OH_TILES]),
                                  num_hi[0:EP, :, :], ALU.is_equal)
                dve.tensor_tensor(oh_lo[0:EP, b, :, :], dst_lo[0:EP, cols].unsqueeze(1).to_broadcast([EP, LO, OH_TILES]),
                                  num_lo[0:EP, :, :], ALU.is_equal).then_inc(S["onehot"], 1)

            onehots(0, 0)
            onehots(1, 1)
            with dve.Fori(1, CHUNKS // 2) as i:
                for b in range(2):
                    dve.wait_ge(S["onehot_used"], 2 * i + b - 1)
                    onehots(2 * i + b, b)

            dve.wait_ge(S["degree"], 1)
            dve.wait_ge(S["gnn_in"], 16 * GNN_LOADS)
            then(dve.tensor_scalar(fw[:, 0, :], bank[0][0:HI, 0:LO], 1.0 / (N - 1), None, ALU.mult))
            then(dve.tensor_tensor(fw[:, 5, :], fw[:, 0, :], noise, ALU.mult))
            dve.tensor_scalar(fw[:, 9, :], fw[:, 0, :], 1e-30, None, ALU.max).then_inc(S["sqrt_in"], 1)
            dve.tensor_scalar(fw[:, 7, :], fw[:, 0, :], 1e-8, None, ALU.add).then_inc(S["dve_step"], 1)
            steps[0] += 1
            dve.wait_ge(S["dve_step"], steps[0])
            dve.scalar_tensor_tensor(fw[:, 1, :], fw[:, 5, :], 0.1, fw[:, 0, :], ALU.mult, ALU.add)
            then(dve.reciprocal(fw[:, 2, :], fw[:, 7, :]))
            dve.wait_ge(S["sqrt_out"], 1)
            then(dve.tensor_tensor(fw[:, 8, :], fw[:, 6, :], fw[:, 6, :], ALU.mult))
            then(dve.tensor_tensor(fw[:, 8, :], fw[:, 0, :], fw[:, 8, :], ALU.subtract))
            then(dve.reciprocal(fw[:, 10, :], fw[:, 6, :]))
            then(dve.tensor_tensor(fw[:, 8, :], fw[:, 8, :], fw[:, 10, :], ALU.mult))
            dve.scalar_tensor_tensor(fw[:, 3, :], fw[:, 8, :], 0.5, fw[:, 6, :], ALU.mult, ALU.add)
            then(dve.memset(fw[:, 4, :], 1.0))
            dve.tensor_scalar(valid[:], node_id[:, 0:1], float(TAIL), None, ALU.is_lt).then_inc(S["feats_ready"], 1)

            def sum_x1(t, j, r):
                dve.wait_ge(S["gnn_ps"], t + 1)
                xr = ring[r][:, j, 0:D]
                dve.tensor_tensor(xr, xr, bank[6 + j % 2][:, 0:D], ALU.add).then_inc(S["x1_ready"], 1)
                dve.wait_ge(S["x1_ready"], t + 1)
                dve.bn_stats(stats[:, j, :], xr).then_inc(S["stats_ready"], 1)

            def norm(g, r, k):
                dve.wait_ge(S["stats_ready"], GROUP * g + GROUP)
                for j in range(GROUP):
                    last = dve.bn_aggr(mv[:, j, :], stats[:, j, :])
                k.then(last)
                dve.tensor_scalar(rt[:, 0, :], mv[:, :, 1], 1.0 + LN_EPS, LN_EPS * LN_EPS, ALU.mult, ALU.add).then_inc(S["var_ready"], 1)

            def refine(g, r, k):
                dve.wait_ge(S["std_ready"], g + 1)
                k.then(dve.reciprocal(rt[:, 2, :], rt[:, 1, :]))
                k.then(dve.tensor_tensor(rt[:, 3, :], rt[:, 2, :], rt[:, 2, :], ALU.mult))
                k.then(dve.tensor_tensor(rt[:, 3, :], rt[:, 3, :], rt[:, 0, :], ALU.mult))
                k.then(dve.tensor_scalar(rt[:, 3, :], rt[:, 3, :], -0.5, 1.5, ALU.mult, ALU.add))
                k.then(dve.tensor_tensor(rstd[:, r, :], rt[:, 3, :], rt[:, 2, :], ALU.mult))
                dve.scalar_tensor_tensor(nmean[:, r, :], mv[:, :, 0], -1.0, rstd[:, r, :], ALU.mult, ALU.mult).then_inc(S["norm_ready"], 1)

            def route(g, r, k, last=False, sent_before=None):
                wide = [P, GROUP, E]
                rev_b = rev[:, :].unsqueeze(1).to_broadcast(wide)
                dve.wait_ge(S["logit_ps"], GROUP * g + GROUP)
                dve.tensor_tensor(lg[:], bank[0][:, 0:GROUP * E].rearrange("p (j e) -> p j e", e=E),
                                  br_bc[:, :].unsqueeze(1).to_broadcast(wide), ALU.add).then_inc(S["logits_read"], 1)
                dve.wait_ge(S["logits_read"], g + 1)
                for best, rank, onehot, of in ((m1, r1, oh1, lg), (m2, r2, oh2, lg2)):
                    k.then(dve.tensor_reduce(best[:], of[:], AX_X, ALU.max))
                    k.then(dve.tensor_tensor(eqm[:], of[:], best[:, :].unsqueeze(2).to_broadcast(wide), ALU.is_equal))
                    k.then(dve.tensor_tensor(eqm[:], eqm[:], rev_b, ALU.mult))
                    k.then(dve.tensor_reduce(rank[:], eqm[:], AX_X, ALU.max))
                    k.then(dve.tensor_tensor(onehot[:], rev_b, rank[:, :].unsqueeze(2).to_broadcast(wide), ALU.is_equal))
                    if of is lg:
                        k.then(dve.scalar_tensor_tensor(lg2[:], oh1[:], -3e38, lg[:], ALU.mult, ALU.add))
                if last:
                    dve.tensor_scalar(oh1[:, GROUP - 1, :], oh1[:, GROUP - 1, :], valid[:], None, ALU.mult)
                    k.then(dve.tensor_scalar(oh2[:, GROUP - 1, :], oh2[:, GROUP - 1, :], valid[:], None, ALU.mult))
                dve.tensor_tensor(both[:, GROUP:2 * GROUP, :], oh1[:], oh2[:], ALU.add).then_inc(S["mask_ready"], 1)
                cols = bass.ds(g * GROUP, GROUP)
                dve.tensor_tensor(gap[:, cols], m2[:], m1[:], ALU.subtract)
                dve.tensor_copy(ring[r][:, :, D], node_id[:, cols])
                dve.tensor_scalar(ring[r][:, :, D + 1], r1[:], -1.0, float(E), ALU.mult, ALU.add)
                dve.wait_ge(S["pos_ps"], g + 1)
                k.then(dve.tensor_tensor(posE[:], bank[1][:, 0:GROUP * E].rearrange("p (j e) -> p j e", e=E),
                                         fill[:, :].unsqueeze(1).to_broadcast(wide), ALU.add))
                k.then(dve.tensor_tensor(fill[:], fill[:], bank[1][:, GROUP * E:(GROUP + 1) * E], ALU.add))
                if sent_before is not None:
                    dve.wait_ge(sent[r], sent_before)
                k.then(dve.tensor_tensor(oh1[:], oh1[:], posE[:], ALU.mult))
                dve.tensor_reduce(dest[:, r, 0, :], oh1[:], AX_X, ALU.add)
                k.then(dve.tensor_tensor(oh2[:], oh2[:], posE[:], ALU.mult))
                dve.tensor_reduce(dest[:, r, 1, :], oh2[:], AX_X, ALU.add).then_inc(S["dest_ready"], 1)

            class Chain:
                def __init__(self, base=None):
                    self.base = base

                def then(self, ins):
                    then(ins, self.base)

            def group(g, r, r_last, k, router=True, sent_before=None):
                for j in range(GROUP):
                    sum_x1(GROUP * g + j, j, r)
                norm(g, r, k)
                if router:
                    route(g - 1, r_last, k, sent_before=sent_before)
                refine(g, r, k)

            dve.wait_ge(S["consts"], 1)
            dve.wait_ge(x_in[0], 16)
            group(0, 0, None, Chain(), router=False)
            dve.wait_ge(x_in[1], 16)
            group(1, 1, 0, Chain())
            dve.wait_ge(x_in[2], 16)
            group(2, 2, 1, Chain())
            dve.wait_ge(x_in[0], 32)
            group(3, 0, 2, Chain())
            dve.wait_ge(x_in[1], 32)
            group(4, 1, 0, Chain(), sent_before=32 * GROUP)
            dve.wait_ge(x_in[2], 32)
            group(5, 2, 1, Chain(), sent_before=32 * GROUP)
            dve.wait_ge(x_in[0], 64)
            group(6, 0, 2, Chain(), sent_before=32 * GROUP)
            k = Chain()
            route(GROUPS - 1, (GROUPS - 1) % RINGS, k, last=True, sent_before=64 * GROUP)

            dve.wait_ge(S["dest_ready"], GROUPS)
            dve.tensor_scalar(pad_dest[:], fill[:], node_id[:, 0:1], None, ALU.add).then_inc(S["fill_ready"], 1)
            k.then(dve.tensor_tensor(jump[:], fill[:], regions[:], ALU.subtract))
            k.then(dve.tensor_scalar(cnt_i[:], jump[:], float(P - 1), None, ALU.add))
            k.then(dve.tensor_scalar(ntile_i[:], cnt_i[:], 7, None, ALU.logical_shift_right))
            dve.memset(cum[:], 0.0)
            k.then(dve.tensor_copy(ntile[:], ntile_i[:]))
            k.then(dve.tensor_copy(cum[:, 0, 4:4 + E], ntile[:]))
            for n, d in enumerate((1, 2, 4)):
                k.then(dve.tensor_tensor(cum[:, (n + 1) % 2, 4:4 + E], cum[:, n % 2, 4:4 + E],
                                         cum[:, n % 2, 4 - d:4 + E - d], ALU.add))
            k.then(dve.tensor_scalar(jump[:], ntile[:], -float(P), float(REGION), ALU.mult, ALU.add))
            wide = [P, SLOT_TILES, E]
            k.then(dve.tensor_tensor(cmp_a, slot_no[:, :].unsqueeze(2).to_broadcast(wide),
                                     cum[:, 1, 4:4 + E].unsqueeze(1).to_broadcast(wide), ALU.is_ge))
            k.then(dve.tensor_reduce(slot_e[:], cmp_a, AX_X, ALU.add))
            dve.tensor_scalar(slot_ei[:], slot_e[:], float(E - 1), None, ALU.min)
            k.then(dve.tensor_tensor(cmp_b, cmp_a, jump[:, :].unsqueeze(1).to_broadcast(wide), ALU.mult))
            k.then(dve.tensor_reduce(slot_f, cmp_b, AX_X, ALU.add))
            dve.scalar_tensor_tensor(slot_row[:], slot_no[:], float(P), slot_f, ALU.mult, ALU.add).then_inc(S["table_ready"], 1)
            dve.memset(valid[:], 0.0).then_inc(S["gap_ready"], 1)

            dve.wait_ge(S["exp_ready"], 1)
            k.then(dve.tensor_scalar(wa[:], wb[:], 1.0, None, ALU.add))
            k.then(dve.reciprocal(wa[:], wa[:]))
            k.then(dve.tensor_tensor(wb[:], wb[:], wa[:], ALU.mult))

            def split_x(s, b, q, in_count, sent_before=None, first=False):
                dve.wait_ge(S["xt_ps"], s + 1)
                if not first:
                    dve.wait_ge(S["h_ps"], s - 1)
                ps = bank[0][:, b * D:(b + 1) * D].rearrange("p (k n) -> p k n", k=KD)
                dve.tensor_copy(xth[:, b, :, :], ps).then_inc(S["xth_ready"], 1)
                dve.wait_ge(xg_in[b], in_count)
                dve.tensor_scalar(y_off[:, b, :], xg[:, b, D + 1:ROW], slot_e[:, bass.ds(s, 1)], float(N),
                                  ALU.not_equal, ALU.mult).then_inc(S["yoff_ready"], 1)
                dve.wait_ge(S["xth_ready"], s + 1)
                dve.tensor_tensor(xtl[:, b, :, :], ps, xth[:, b, :, :].bitcast(F32), ALU.subtract).then_inc(S["xt_ready"], 1)
                if sent_before is not None:
                    dve.wait_ge(y_sent[b], sent_before)
                dve.wait_ge(S["yoff_ready"], s + 1)
                dve.tensor_tensor(y_row[:, q, :], y_off[:, b, :], xg[:, b, D:D + 1], ALU.add).then_inc(S["yrow_ready"], 1)

            def low_ht(s, b, first=False):
                dve.wait_ge(S["hth_ready"], s + 1)
                dve.tensor_tensor(htl[:, b, :, :], bank[3 + b][:, :].rearrange("p (k n) -> p k n", k=KH),
                                  hth[:, b, :, :].bitcast(F32), ALU.subtract).then_inc(S["htl_ready"], 1)

            split_x(0, 0, 0, 16, first=True)
            split_x(1, 1, 1, 16, first=True)
            split_x(2, 0, 2, 32)
            low_ht(0, 0)
            split_x(3, 1, 3, 32)
            low_ht(1, 1)
            with dve.Fori(1, SLOT_TILES // 4) as i:
                for q in range(4):
                    split_x(4 * i + q, q % 2, q, 16 * (2 * i + q // 2 + 1), 16 * (2 * i + q // 2 - 1))
                    low_ht(4 * i + q - 2, q % 2)
            split_x(SLOT_TILES - 1, 0, 0, 16 * (SLOT_TILES // 2 + 1), 16 * (SLOT_TILES // 2 - 1))
            for s in range(SLOT_TILES - 3, SLOT_TILES):
                low_ht(s, s % 2)

            dve.wait_ge(S["x1_back"], 16)
            for g in range(GROUPS):
                dve.wait_ge(y_back[g], 32 if g + 1 < GROUPS else 64)
                for k2, (w, done) in enumerate(((wa, "half_summed"), (wb, "summed"))):
                    part = y_parts(g)[k2].rearrange("p j d -> p (j d)")
                    if k2:
                        dve.wait_ge(S["half_summed"], GROUP * (g + 1))
                    with dve.Fori(0, GROUP) as j:
                        xr = arena[:, bass.ds((g * GROUP + j) * D, D)]
                        dve.scalar_tensor_tensor(xr, part[:, bass.ds(j * D, D)], w[:, bass.ds(g * GROUP + j, 1)], xr,
                                                 ALU.mult, ALU.add).then_inc(S[done], 1)

        @block.tensor
        def _(pe):
            pe.wait_ge(S["zeroed"], 1)
            zero_b = zeros[:, :].bitcast(BF16)
            pe.matmul(bank[0][0:HI, 0:LO], zero_b[0:EP, 0:HI], zero_b[0:EP, 0:LO], start=True, stop=False)
            pe.matmul(bank[1][0:E, 0:H], zero_b[:, 0:E], zero_b[:, 0:H], start=True, stop=False).then_inc(S["beta_w1"], 1)

            def count(c, b):
                pe.wait_ge(S["onehot"], c + 1)
                for t in range(OH_TILES):
                    mm = pe.matmul(bank[0][0:HI, 0:LO], oh_hi[0:EP, b, :, t], oh_lo[0:EP, b, :, t], start=False, stop=False)
                mm.then_inc(S["onehot_used"], 1)

            with pe.Fori(0, E) as e:
                for c in range(6):
                    count(6 * e + c, c % 2)
                pe.wait_ge(S["stage_a"], 16 * e + 16)
                pe.wait_ge(S["beta_now"], e + 1)
                for k in range(KD):
                    mm = pe.matmul(bank[1][0:E, 0:H], beta_now[:, k, :], stage_w1[:, k, :], start=False, stop=False)
                mm.then_inc(S["beta_w1"], 1)
            for c in range(6 * E, CHUNKS):
                count(c, c % 2)
            pe.matmul(bank[0][0:HI, 0:LO], zero_b[0:EP, 0:HI], zero_b[0:EP, 0:LO], start=False, stop=True).then_inc(S["degree"], 1)
            pe.matmul(bank[1][0:E, 0:H], zero_b[:, 0:E], zero_b[:, 0:H], start=False, stop=True).then_inc(S["bias_ps"], 1)
            pe.wait_ge(S["gnn_in"], 16 * GNN_LOADS)
            for k in range(KD):
                mm = pe.matmul(bank[2][0:5, 0:D], vec_w[:, k, :], w1g[:, k, :], start=(k == 0), stop=(k == KD - 1))
            mm.then_inc(S["mix_ps"], 1)
            pe.wait_ge(S["beta_ready"], 2 * KD)
            for k in range(KD):
                mm = pe.matmul(bank[3][:, 0:E], beta_bc[:, k, :], wr_raw[:, k, :], start=(k == 0), stop=(k == KD - 1))
            mm.then_inc(S["mix_ps"], 1)

            def hidden(t, j, r, first=False):
                if not (first and j < 2):
                    pe.wait_ge(S["hid_ready"], t - ring_step(j) + 1)
                for k in range(KD):
                    mm = pe.matmul(bank[4 + j % 2][:, k * P:(k + 1) * P], mix[:, k * P:(k + 1) * P],
                                   feat[:, r, j * P:(j + 1) * P], start=True, stop=True)
                mm.then_inc(S["hid_ps"], 1)

            def gnn_out(t, j, first=False):
                pe.wait_ge(S["hid_ready"], t + 1)
                if not (first and j < 2):
                    pe.wait_ge(S["x1_ready"], t - ring_step(j) + 1)
                o = bank[6 + j % 2][:, 0:D]
                pe.matmul(o, sel[:, 0, :], b2g, start=True, stop=False)
                for k in range(KD):
                    mm = pe.matmul(o, g_t[:, j % 2, k, :], w2g[:, k, :], start=False, stop=(k == KD - 1))
                mm.then_inc(S["gnn_ps"], 1)

            def turn_u(t, j, r, first=False):
                pe.wait_ge(S["u_ready"], t + 1)
                if not (first and j < 2):
                    pe.wait_ge(S["ut_ready"], t - ring_step(j) + 1)
                for k in range(KD):
                    mm = pe.transpose(bank[2 + j % 2][:, k * P:(k + 1) * P], ring[r][:, j, k * P:(k + 1) * P], ident[:, :])
                mm.then_inc(S["ut_ps"], 1)

            def logits(t, j):
                pe.wait_ge(S["ut_ready"], t + 1)
                for k in range(KD):
                    mm = pe.matmul(bank[0][:, j * E:(j + 1) * E], u_t[:, j % 2, k, :], wr_g[:, k, :],
                                   start=(k == 0), stop=(k == KD - 1))
                mm.then_inc(S["logit_ps"], 1)

            def places(g):
                pe.wait_ge(S["mask_ready"], g + 1)
                m = both[:, :, :].rearrange("p j e -> p (j e)")
                for d in range(GROUP + 1):
                    mm = pe.matmul(bank[1][:, 0:(GROUP + 1) * E], (ones if d else below)[:, :],
                                   m[:, (GROUP - d) * E:(2 * GROUP + 1 - d) * E], start=(d == 0), stop=(d == GROUP))
                mm.then_inc(S["pos_ps"], 1)

            def group(g, r, r_last, f, has_hidden=True, router=True, first=False, second=False):
                for j in range(GROUP + 1):
                    if j < GROUP:
                        if has_hidden:
                            hidden(GROUP * g + j, j, f, first)
                        if router:
                            turn_u(GROUP * (g - 1) + j, j, r_last, second)
                    if j >= 1:
                        if has_hidden:
                            gnn_out(GROUP * g + j - 1, j - 1, first)
                        if router:
                            if j == 1 and not second:
                                pe.wait_ge(S["logits_read"], g - 1)
                            logits(GROUP * (g - 1) + j - 1, j - 1)
                if router:
                    places(g - 1)

            pe.wait_ge(S["mix_ready"], 1)
            pe.wait_ge(S["beta_b1"], 1)
            pe.wait_ge(S["mix_copied"], 2)
            pe.wait_ge(S["prep_done"], 1)
            pe.wait_ge(S["consts"], 1)
            pe.wait_ge(S["wrg_ready"], KD)
            for g in range(GROUPS):
                pe.wait_ge(feat_in[g % 2], 16 * (g // 2 + 1))
                group(g, g % RINGS, (g - 1) % RINGS, g % 2, router=g > 0, first=g == 0, second=g == 1)
            group(GROUPS, None, (GROUPS - 1) % RINGS, None, has_hidden=False)

            def turn_x(s, b, in_count, first=False):
                pe.wait_ge(xg_in[b], in_count)
                if not first:
                    pe.wait_ge(S["xt_ready"], s - 1)
                for k in range(KD):
                    mm = pe.transpose(bank[0][:, b * D + k * P:b * D + (k + 1) * P], xg[:, b, k * P:(k + 1) * P], ident[:, :])
                mm.then_inc(S["xt_ps"], 1)

            def layer1(s, b, first=False):
                e = pe.value_load(slot_ei[0:1, bass.ds(s, 1)], min_val=0, max_val=E - 1)
                pe.wait_ge(S["xt_ready"], s + 1)
                if not first:
                    pe.wait_ge(S["h_ready"], s - 1)
                o = bank[1 + b][:, :]
                pe.matmul(o, sel[:, :, :].rearrange("p e m -> p (e m)")[:, bass.ds(e * P, P)], b1s[:, :], start=True, stop=False)
                for k in range(KD):
                    high = w1h[:, bass.ds(e * (KD * H) + k * H, H)]
                    low = w1l[:, bass.ds(e * (KD * H) + k * H, H)]
                    pe.matmul(o, xth[:, b, k, :], high, start=False, stop=False)
                    pe.matmul(o, xth[:, b, k, :], low, start=False, stop=False)
                    mm = pe.matmul(o, xtl[:, b, k, :], high, start=False, stop=(k == KD - 1))
                mm.then_inc(S["h_ps"], 1)
                return e

            def turn_h(s, b, first=False):
                pe.wait_ge(S["h_ready"], s + 1)
                if not first:
                    pe.wait_ge(S["htl_ready"], s - 1)
                for k in range(KH):
                    mm = pe.transpose(bank[3 + b][:, k * P:(k + 1) * P], hbuf[:, b, k * P:(k + 1) * P], ident[:, :])
                mm.then_inc(S["ht_ps"], 1)

            def layer2(s, b, first=False):
                e = pe.value_load(slot_ei[0:1, bass.ds(s, 1)], min_val=0, max_val=E - 1)
                pe.wait_ge(S["htl_ready"], s + 1)
                if not first:
                    pe.wait_ge(S["y_ready"], s - 1)
                o = bank[5 + b][:, 0:D]
                pe.matmul(o, sel[:, :, :].rearrange("p e m -> p (e m)")[:, bass.ds(e * P, P)], b2s[:, :], start=True, stop=False)
                for k in range(KH):
                    high = w2h[:, bass.ds(e * (KH * D) + k * D, D)]
                    low = w2l[:, bass.ds(e * (KH * D) + k * D, D)]
                    pe.matmul(o, hth[:, b, k, :], high, start=False, stop=False)
                    pe.matmul(o, hth[:, b, k, :], low, start=False, stop=False)
                    mm = pe.matmul(o, htl[:, b, k, :], high, start=False, stop=(k == KH - 1))
                mm.then_inc(S["y_ps"], 1)

            pe.wait_ge(S["table_ready"], 1)
            turn_x(0, 0, 16, first=True)
            layer1(0, 0, first=True)
            turn_x(1, 1, 16, first=True)
            layer1(1, 1, first=True)
            turn_x(2, 0, 32)
            turn_h(0, 0, first=True)
            layer1(2, 0)
            turn_x(3, 1, 32)
            turn_h(1, 1, first=True)
            layer2(0, 0, first=True)
            layer1(3, 1)
            turn_x(4, 0, 48)
            turn_h(2, 0)
            layer2(1, 1, first=True)
            with pe.Fori(2, SLOT_TILES // 2) as i:
                for b in range(2):
                    layer1(2 * i + b, b)
                    turn_x(2 * i + b + 1, 1 - b, 16 * (i + 1 + b))
                    turn_h(2 * i + b - 1, 1 - b)
                    layer2(2 * i + b - 2, b)
            layer1(SLOT_TILES - 1, 0)
            turn_h(SLOT_TILES - 2, 1)
            layer2(SLOT_TILES - 3, 0)
            turn_h(SLOT_TILES - 1, 0)
            layer2(SLOT_TILES - 2, 1)
            layer2(SLOT_TILES - 1, 0)


_INS = ["x", "dst", "node_vec", "L0_gnn_W_deg", "L0_gnn_b_deg", "L0_gnn_W_bet", "L0_gnn_b_bet", "L0_gnn_W_clo",
        "L0_gnn_b_clo", "L0_gnn_W_eig", "L0_gnn_b_eig", "L0_gnn_W1", "L0_gnn_b1", "L0_gnn_W2", "L0_gnn_b2",
        "L0_ffn_gamma", "L0_ffn_beta", "L0_ffn_Wr", "L0_ffn_br", "L0_ffn_W1", "L0_ffn_b1", "L0_ffn_W2", "L0_ffn_b2"]


def kernel(**inputs):
    import numpy as _np
    import concourse.bacc as _bacc
    from concourse import mybir as _mybir
    from concourse.bass_utils import run_bass_kernel_spmd as _run

    nc = _bacc.Bacc("TRN2", target_bir_lowering=False, num_devices=1)
    arrays, args = {}, []
    for name in _INS:
        a = _np.ascontiguousarray(inputs[name])
        arrays[f"in_{name}_dram"] = a
        args.append(nc.dram_tensor(f"in_{name}_dram", a.shape, _mybir.dt.from_np(a.dtype), kind="ExternalInput").ap())
    args.append(nc.dram_tensor("out_0_dram", inputs["x"].shape, _mybir.dt.float32, kind="ExternalOutput").ap())
    gnn_ffn_kernel(nc, *args)
    r = _run(nc, [arrays], core_ids=[0])
    return r.results[0]["out_0_dram"]
```

```python
from contextlib import ExitStack

import concourse.bass as bass
from concourse import mybir

ALU = mybir.AluOpType
ACT = mybir.ActivationFunctionType
AX_X = mybir.AxisListType.X
F32 = mybir.dt.float32
F32R = mybir.dt.float32r
BF16 = mybir.dt.bfloat16
I32 = mybir.dt.int32
U32 = mybir.dt.uint32

P = 128
LN_EPS = 1e-5

LO = 64
OH_TILES = 16

GROUP = 7
RINGS = 5

TILE = 256

U_SLOT = 10
ROUTE_SLOT = 15
PLACE_SLOT = 18

GNN_LOADS = 15

SIGNALS = """
    dst_in small_in gnn_in zeroed numbers consts prep_done spare_sent bias_moved rows_zeroed
    beta_bc_ready beta_w1 w1_in b1_in b1_ready b2_in mix_ps mix_copied mix_ready wrg_ready
    w2_high w2_low onehot onehot_used degree sqrt_in sqrt_out feats_ready feat_kept
    pool_step dve_step
    hid_ps hid_ready gnn_ps x1_ready stats_ready var_ready std_ready norm_ready
    u_ready ut_ps ut_ready logit_ps logits_read mask_ready pos_ps dest_ready fill_ready table_ready
    pads_sent wcur_high wcur_ready
    xt_ps xth_ready xt_ready meta_step meta_ready tanh_ready weight_ready h_ps h_ready hth_ready htl_ready
    y_ps yb_ready y_ready y_sent carried
""".split()


def later(s, d):
    return not isinstance(s, int) or s >= d


def gnn_ffn_kernel(nc, x, dst, node_vec, g_wdeg, g_bdeg, g_wbet, g_bbet, g_wclo, g_bclo, g_weig, g_beig,
                   g_w1, g_b1, g_w2, g_b2, gamma, beta, wr, br, w1, b1, w2, b2, out):
    N, D = x.shape
    E, _, H = w1.shape
    n_edges = dst.shape[0]
    KD, KH = D // P, H // P
    EW = KD * H
    TILES = -(-N // P)
    TAIL = N - (TILES - 1) * P
    GROUPS = TILES // GROUP
    assert GROUPS * GROUP == TILES and RINGS < GROUPS <= RINGS + 2 and D == 256 and H == 512 and E == 8
    assert KH * D == EW
    NPAD = TILES * P
    HI = NPAD // LO
    EP = 125
    ECOLS = n_edges // EP
    CHUNKS = ECOLS // OH_TILES
    assert EP * ECOLS == n_edges and CHUNKS * OH_TILES == ECOLS and CHUNKS % 2 == 0
    REGION = NPAD + TILE
    ROW = D + 3
    SLOT_TILES = (2 * N + E * (TILE - 1)) // TILE
    SPARE_AT = E * REGION
    assert SLOT_TILES % 4 == 0

    with ExitStack() as ctx:
        def sb(name, shape, dt):
            return ctx.enter_context(nc.sbuf_tensor(name, shape, dt))

        def sem(name):
            return ctx.enter_context(nc.semaphore(name))

        ctx.enter_context(nc.allow_low_precision(reason="sums of row numbers are exact integers in float32"))
        ctx.enter_context(nc.allow_non_contiguous_dma(reason="a few short vectors are laid over partitions"))

        feat_dram = nc.dram_tensor("feat_dram", (5, NPAD), F32).ap()
        routed = nc.dram_tensor("routed", (SPARE_AT + TILE, ROW), F32).ap()

        w1r = sb("w1r", [P, E * EW], F32)
        w2h = sb("w2h", [P, E * EW], F32R)
        w2l = sb("w2l", [P, E * EW], F32R)
        b1t = sb("b1t", [P, E * KH], F32)
        b1_raw = sb("b1_raw", [P, E * KH], F32)
        three = sb("three", [P, P], BF16)
        ident = sb("ident", [P, P], F32)
        below = sb("below", [P, P], BF16)
        ones = sb("ones", [P, P], BF16)
        wr_g = sb("wr_g", [P, KD, E], F32)
        br_bc = sb("br_bc", [P, E], F32)
        br_raw = sb("br_raw", [P, E], F32)
        rev = sb("rev", [P, E], F32)
        node_id = sb("node_id", [P, TILES], F32)
        fill = sb("fill", [P, E], F32)
        regions = sb("regions", [P, E], F32)
        slot_no = sb("slot_no", [P, SLOT_TILES], F32)
        slot_e = sb("slot_e", [P, SLOT_TILES], F32)
        slot_ei = sb("slot_ei", [P, SLOT_TILES], I32)
        slot_row = sb("slot_row", [P, SLOT_TILES], I32)
        pad_rows = sb("pad_rows", [P, 2, ROW], F32)
        zeros = pad_rows[:, 0, 0:D]
        fence = sb("fence", [P, 1], F32)

        xg = sb("xg", [P, 2, 2, ROW], F32)
        xth = sb("xth", [P, 2, KD, TILE], F32R)
        xtl = sb("xtl", [P, 2, KD, TILE], F32R)
        hbuf = sb("hbuf", [P, 2, KH, TILE], F32)
        hth = sb("hth", [P, 2, KH, TILE], F32R)
        htl = sb("htl", [P, 2, KH, TILE], F32R)
        w1cur = sb("w1cur", [P, 2, 2, EW], F32R)
        b1cur = sb("b1cur", [P, 2, KH], F32)
        y_row = sb("y_row", [P, 4, 2], U32)
        lead = sb("lead", [P, 2, 2, 2], F32)
        half_tanh = sb("half_tanh", [P, 2, 2], F32)
        weight = sb("weight", [P, 4, 2], F32)
        stage = [hbuf[:, b, :, :].rearrange("p k n -> p (k n)") for b in range(2)]

        gb = sb("gb", [P, 2, KD], F32)
        stats = sb("stats", [P, 2, GROUP, 6], F32)
        mv = sb("mv", [P, GROUP, 2], F32)
        rt = sb("rt", [P, 4, GROUP], F32)
        rstd = sb("rstd", [P, RINGS, GROUP], F32)
        nmean = sb("nmean", [P, RINGS, GROUP], F32)
        lg = sb("lg", [P, GROUP, E], F32)
        lg2 = sb("lg2", [P, GROUP, E], F32)
        eqm = sb("eqm", [P, GROUP, E], F32)
        oh1 = sb("oh1", [P, GROUP, E], F32)
        oh2 = sb("oh2", [P, GROUP, E], F32)
        both = sb("both", [P, 2 * GROUP + 1, E], BF16)
        posE = sb("posE", [P, GROUP, E], F32)
        m1 = sb("m1", [P, GROUP], F32)
        m2 = sb("m2", [P, GROUP], F32)
        r1 = sb("r1", [P, GROUP], F32)
        r2 = sb("r2", [P, GROUP], F32)
        valid = sb("valid", [P, 1], F32)
        dest = sb("dest", [P, RINGS, 2, GROUP], U32)
        pad_at = sb("pad_at", [P, E], I32)
        cnt_i = sb("cnt_i", [P, E], I32)
        ntile_i = sb("ntile_i", [P, E], I32)
        ntile = sb("ntile", [P, E], F32)
        cum = sb("cum", [P, 2, 4 + E], F32)
        jump = sb("jump", [P, E], F32)

        ARENA = 13184
        arena = sb("arena", [P, ARENA], F32)

        def view(at, words):
            assert at + words <= ARENA
            return arena[:, at:at + words]

        RW = GROUP * ROW
        ring = [view(r * RW, RW).rearrange("p (j r) -> p j r", r=ROW) for r in range(RINGS)]
        at_feat = RINGS * RW
        at_ut = at_feat + 2 * GROUP * P
        at_gt = at_ut + 2 * D
        at_w2g = at_gt + 2 * D
        at_mix = at_w2g + KD * D
        at_small = at_mix + D
        feat = view(at_feat, 2 * GROUP * P).rearrange("p (b n) -> p b n", b=2)
        u_t = view(at_ut, 2 * D).rearrange("p (b k n) -> p b k n", b=2, k=KD)
        g_t = view(at_gt, 2 * D).rearrange("p (b k n) -> p b k n", b=2, k=KD)
        w2g = view(at_w2g, KD * D).rearrange("p (k d) -> p k d", k=KD)
        mix = view(at_mix, D)
        b2g = view(at_small, D // 2).bitcast(BF16)
        noise = view(at_small + D // 2, LO)[0:HI, :]
        wr_raw = view(at_small + D // 2 + LO, KD * E).rearrange("p (k e) -> p k e", k=KD)
        vec_w = view(at_small + D // 2 + LO + KD * E, KD * 5).rearrange("p (k q) -> p k q", k=KD)
        beta_bc = view(at_small + D // 2 + LO + KD * E + KD * 5, KD * P).rearrange("p (k m) -> p k m", k=KD)
        w1g = view(at_ut, KD * D).rearrange("p (k d) -> p k d", k=KD)
        fw = view(at_feat, 12 * LO)[0:HI, :].rearrange("p (f l) -> p f l", f=12)
        bias_f = view(at_feat + 12 * LO, D)[0:1, :]
        bias_p = view(at_feat + 12 * LO + D, 3 * D // 2).bitcast(BF16).rearrange("p (q n) -> p q n", q=3)[0:1, :, :]
        mix_bias = xg[0:5, 0, 0, 0:D]
        used = [RW]

        def hist(words):
            used[0] += words
            assert used[0] <= RINGS * RW
            return view(used[0] - words, words)

        oh_hi = hist(2 * HI * OH_TILES // 2).bitcast(BF16).rearrange("p (b j t) -> p b j t", b=2, t=OH_TILES)
        oh_lo = hist(2 * LO * OH_TILES // 2).bitcast(BF16).rearrange("p (b j t) -> p b j t", b=2, t=OH_TILES)
        num_hi = hist(HI * OH_TILES // 2).bitcast(BF16).rearrange("p (j t) -> p j t", t=OH_TILES)
        num_lo = hist(LO * OH_TILES // 2).bitcast(BF16).rearrange("p (j t) -> p j t", t=OH_TILES)
        dst_hi = hist(ECOLS // 2).bitcast(BF16)
        dst_lo = hist(ECOLS // 2).bitcast(BF16)
        dst_i = hist(ECOLS).bitcast(I32)
        hi_i = hist(ECOLS).bitcast(I32)
        lo_i = hist(ECOLS).bitcast(I32)
        at_b2 = 3 * RW
        at_cmp = at_gt
        assert at_b2 + E * D <= RINGS * RW
        ybuf = view(0, 4 * D).rearrange("p (b h d) -> p b h d", b=2, h=2)
        b2_bc = view(at_b2, E * D)
        cmp_a = view(at_cmp, SLOT_TILES * E).rearrange("p (s e) -> p s e", e=E)
        cmp_b = view(at_cmp + SLOT_TILES * E, SLOT_TILES * E).rearrange("p (s e) -> p s e", e=E)
        slot_f = view(at_cmp + 2 * SLOT_TILES * E, SLOT_TILES)

        bank = [ctx.enter_context(nc.psum_tensor(f"bank{i}", [P, 512], F32)) for i in range(8)]

        S = {}
        for name in SIGNALS:
            S[name] = sem("s_" + name)
        x_in = [sem(f"s_x_in{r}") for r in range(RINGS)]
        feat_in = [sem(f"s_feat_in{r}") for r in range(2)]
        x1_kept = [sem(f"s_x1_kept{q}") for q in range(2)]
        sent = [sem(f"s_sent{r}") for r in range(RINGS)]
        stage_w2 = [sem(f"s_stage_w2_{b}") for b in range(2)]
        xg_in = [sem(f"s_xg_in{r}") for r in range(2)]

        block = ctx.enter_context(nc.Block())

        w2_dram = w2.rearrange("e (k p) d -> e p k d", p=P)

        def node_parts(dram, first, count):
            whole = count if first + count < TILES else count - 1
            parts = [(P, slice(0, whole), dram[first * P:(first + whole) * P, :].rearrange("(j p) d -> p j d", p=P))]
            if whole < count:
                parts.append((TAIL, whole, dram[(first + whole) * P:N, :]))
            return parts

        FIRST_PART = 4

        def store_of(t):
            g, j = divmod(t, GROUP)
            return (0, 16 * g + 16) if j < FIRST_PART else (1, 16 * g + (16 if g + 1 < GROUPS else 32))

        def u_tiles(slot):
            found = []
            for g in range(GROUPS):
                n = slot - GROUP * g - U_SLOT
                if 0 <= n < (GROUP + 1) // 2:
                    found += [GROUP * g + j for j in (2 * n, 2 * n + 1) if j < GROUP]
            return found

        LAST_SLOT = GROUP * (GROUPS - 1) + PLACE_SLOT

        @block.sync
        def _(sp):
            sp.dma_start(dst_i[0:EP, :], dst.rearrange("(p c) -> p c", c=ECOLS)).then_inc(S["dst_in"], 16)
            sp.dma_start(gb[:, 0, :], gamma.rearrange("(k p) -> p k", p=P)).then_inc(S["small_in"], 16)
            sp.dma_start(gb[:, 1, :], beta.rearrange("(k p) -> p k", p=P)).then_inc(S["small_in"], 16)
            for b in range(2):
                sp.dma_start(stage[b].rearrange("p (k d) -> p k d", k=KH), w2_dram[b]).then_inc(stage_w2[b], 16)
            sp.dma_start(wr_raw, wr.rearrange("(k p) e -> p k e", p=P)).then_inc(S["gnn_in"], 16)
            sp.dma_start(w1g, g_w1.rearrange("(k p) h -> p k h", p=P)).then_inc(S["gnn_in"], 16)
            sp.dma_start(w2g, g_w2.rearrange("(k p) h -> p k h", p=P)).then_inc(S["gnn_in"], 16)
            sp.wait_ge(S["zeroed"], 1)
            for q, (wv, bv) in enumerate([(g_wdeg, g_bdeg), (g_wbet, g_bbet), (g_wclo, g_bclo), (g_weig, g_beig)]):
                rows = slice(64 * (q % 2), 64 * (q % 2) + 64)
                sp.dma_start(vec_w[rows, q // 2, q:q + 1], wv.rearrange("(p a) -> p a", a=1)).then_inc(S["gnn_in"], 16)
                sp.dma_start(vec_w[rows, q // 2, 4:5], bv.rearrange("(p a) -> p a", a=1)).then_inc(S["gnn_in"], 16)
            sp.dma_start(mix_bias[4:5, :], g_b1.rearrange("(a d) -> a d", a=1)).then_inc(S["gnn_in"], 16)
            sp.dma_start(noise[0:HI - 1, :], node_vec[0:(HI - 1) * LO].rearrange("(h l) -> h l", l=LO)).then_inc(S["gnn_in"], 16)
            sp.dma_start(noise[HI - 1:HI, 0:N - (HI - 1) * LO],
                         node_vec[(HI - 1) * LO:N].rearrange("(a l) -> a l", a=1)).then_inc(S["gnn_in"], 16)
            sp.dma_start(br_raw[:], br.rearrange("(a e) -> a e", a=1).to_broadcast([P, E])).then_inc(S["gnn_in"], 16)
            for m in range(KH):
                sp.dma_start(b1_raw[:, :].rearrange("p (e m) -> p e m", m=KH)[:, :, m],
                             b1.rearrange("e (m p) -> m p e", p=P)[m]).then_inc(S["b1_in"], 16)
            sp.dma_start(out[N:N + TILE, :].rearrange("(p h) d -> p h d", h=2), pad_rows[:, :, 0:D]).then_inc(S["rows_zeroed"], 16)
            sp.dma_start(routed[SPARE_AT:SPARE_AT + TILE, :].rearrange("(p h) r -> p h r", h=2), pad_rows[:]).then_inc(S["spare_sent"], 16)

            def load_x(g):
                for rows, j, part in node_parts(x, GROUP * g, GROUP):
                    sp.dma_start(ring[g % RINGS][0:rows, j, 0:D], part).then_inc(x_in[g % RINGS], 16)

            def load_features(g):
                sp.dma_start(feat[0:5, g % 2, :], feat_dram[:, g * GROUP * P:(g + 1) * GROUP * P]).then_inc(feat_in[g % 2], 16)

            load_x(0)
            with sp.Fori(1, E // 2) as i:
                for b in range(2):
                    sp.wait_ge(S["w2_low"], 2 * i + b - 1)
                    sp.dma_start(stage[b].rearrange("p (k d) -> p k d", k=KH),
                                 w2_dram[bass.ds(2 * i + b, 1)].rearrange("a p k d -> p (a k) d")).then_inc(stage_w2[b], 16)
            for k in range(KD):
                sp.dma_start(w1r[:, :].rearrange("p (e k h) -> p e k h", e=E, k=KD)[:, :, k, :],
                             w1[:, k * P:(k + 1) * P, :].rearrange("e p h -> p e h")).then_inc(S["w1_in"], 16)

            sp.wait_ge(S["feats_ready"], 1)
            sp.dma_start(feat_dram.rearrange("f (h l) -> h f l", l=LO), fw[:, 0:5, :]).then_inc(S["feat_kept"], 16)
            load_x(1)
            sp.wait_ge(S["feat_kept"], 16)
            sp.wait_ge(S["prep_done"], 1)
            load_features(0)
            load_features(1)
            for g in range(2, RINGS):
                load_x(g)
            for g in range(GROUPS):
                for q, (first, count) in enumerate(((0, FIRST_PART), (FIRST_PART, GROUP - FIRST_PART))):
                    sp.wait_ge(S["x1_ready"], GROUP * g + first + count)
                    for rows, j, part in node_parts(out[0:N, :], GROUP * g + first, count):
                        src = ring[g % RINGS][0:rows, first + j, 0:D] if isinstance(j, int) else \
                            ring[g % RINGS][0:rows, first + j.start:first + j.stop, 0:D]
                        sp.dma_start(part, src).then_inc(x1_kept[q], 16)
                if g + 2 < GROUPS:
                    sp.wait_ge(S["hid_ps"], GROUP * (g + 1))
                    load_features(g + 2)
                if g >= 3 and g + 2 < GROUPS:
                    sp.wait_ge(sent[g - 3], 32 * GROUP)
                    load_x(g + 2)

            sp.wait_ge(sent[3], 32 * GROUP)
            sp.wait_ge(sent[4], 32 * GROUP)
            sp.dma_start(b2_bc, b2.rearrange("e d -> (e d)").rearrange("(a n) -> a n", a=1).to_broadcast([P, E * D])).then_inc(S["b2_in"], 16)
            sp.wait_ge(S["fill_ready"], 1)
            for e in range(E):
                row = sp.value_load(pad_at[0:1, e:e + 1], min_val=0, max_val=SPARE_AT - TILE)
                sp.dma_start(routed[bass.ds(row, TILE), :].rearrange("(p h) r -> p h r", h=2), pad_rows[:]).then_inc(S["pads_sent"], 16)

            def load_slot(s, b):
                row = sp.value_load(slot_row[0:1, bass.ds(s, 1)], min_val=0, max_val=SPARE_AT)
                sp.dma_start(xg[:, b, :, :], routed[bass.ds(row, TILE), :].rearrange("(p h) r -> p h r", h=2)).then_inc(xg_in[b], 16)

            sp.wait_ge(S["table_ready"], 1)
            for r in range(RINGS):
                sp.wait_ge(sent[r], 32 * GROUP * len(range(r, GROUPS, RINGS)))
            sp.wait_ge(S["pads_sent"], 16 * E)
            sp.wait_ge(S["spare_sent"], 16)
            load_slot(0, 0)
            load_slot(1, 1)
            with sp.Fori(1, SLOT_TILES // 2) as i:
                for b in range(2):
                    sp.wait_ge(S["meta_ready"], 2 * i + b - 1)
                    sp.wait_ge(S["xt_ps"], 2 * i + b - 1)
                    load_slot(2 * i + b, b)
            sp.wait_ge(S["y_sent"], 32 * SLOT_TILES)
            for t in (TILES - GROUP, TILES - 1):
                q, count = store_of(t)
                sp.wait_ge(x1_kept[q], count)
            sp.wait_ge(S["rows_zeroed"], 16)

        @block.gpsimd
        def _(pool):
            steps = [0]

            def then(ins):
                steps[0] += 1
                ins.then_inc(S["pool_step"], 1)
                pool.wait_ge(S["pool_step"], steps[0])

            for q, (t, n) in enumerate([(num_hi, HI), (num_lo, LO)]):
                pool.iota(t, pattern=[[1, n], [0, OH_TILES]], base=0, channel_multiplier=0,
                          allow_small_or_imprecise_dtypes=True).then_inc(S["numbers"], 1)
            then(pool.memset(vec_w, 0.0))
            then(pool.memset(mix_bias, 0.0))
            then(pool.memset(noise, 0.0))
            then(pool.memset(pad_rows[:], 0.0))
            then(pool.iota(pad_rows[:, :, D], pattern=[[1, 2]], base=N, channel_multiplier=2,
                           allow_small_or_imprecise_dtypes=True))
            then(pool.memset(pad_rows[:, :, D + 1], -1.0))
            pool.memset(fence[:], 0.0).then_inc(S["zeroed"], 1)
            pool.wait_ge(S["small_in"], 32)

            with pool.Fori(0, E // 2) as i:
                for b in range(2):
                    e = 2 * i + b
                    pool.wait_ge(S["w2_high"], e + 1)
                    at = bass.ds(e * EW, EW)
                    pool.tensor_tensor(w2l[:, at], stage[b], w2h[:, at].bitcast(F32), ALU.subtract).then_inc(S["w2_low"], 1)

            for k in range(KD):
                pool.tensor_copy(beta_bc[:, k, :], gb[:, 1, k:k + 1].to_broadcast([P, P])).then_inc(S["beta_bc_ready"], 1)
            then(pool.memset(ident[:], 0.0))
            then(pool.affine_select(out=ident[:], in_=ident[:], compare_op=ALU.not_equal, fill=1.0, base=0,
                                    pattern=[[-1, P]], channel_multiplier=1))
            then(pool.memset(ones[:], 1.0))
            then(pool.affine_select(out=below[:], in_=ones[:], compare_op=ALU.is_gt, fill=0.0, base=0,
                                    pattern=[[1, P]], channel_multiplier=-1))
            then(pool.memset(three[:], 0.0))
            for part in range(3):
                then(pool.affine_select(out=three[:], in_=three[:], compare_op=ALU.not_equal, fill=1.0, base=-32 * part,
                                        pattern=[[0, P]], channel_multiplier=1))
            for t, step, n, base, per_row in ((rev, -1, E, E, 0), (fill, REGION, E, 0, 0), (regions, REGION, E, 0, 0),
                                              (node_id, P, TILES, 0, 1), (slot_no, 1, SLOT_TILES, 0, 0)):
                then(pool.iota(t[:], pattern=[[step, n]], base=base, channel_multiplier=per_row,
                               allow_small_or_imprecise_dtypes=True))
            then(pool.memset(both[:], 0.0))
            then(pool.memset(b2g, 0.0))
            pool.dma_start(bias_f, g_b2.rearrange("(a d) -> a d", a=1)).then_inc(S["bias_moved"], 16)
            pool.wait_ge(S["bias_moved"], 16)
            then(pool.tensor_copy(bias_p[:, 0, :], bias_f))
            for q in range(2):
                then(pool.tensor_tensor(bias_f, bias_f, bias_p[:, q, :], ALU.subtract))
                then(pool.tensor_copy(bias_p[:, q + 1, :], bias_f))
            for q in range(3):
                pool.dma_start(b2g[32 * q:32 * q + 1, :], bias_p[:, q, :]).then_inc(S["bias_moved"], 16)
            pool.wait_ge(S["bias_moved"], 64)
            pool.memset(fence[:], 0.0).then_inc(S["consts"], 1)
            pool.wait_ge(S["mix_copied"], 2)
            pool.tensor_tensor(mix[0:5, :], mix[0:5, :], mix_bias, ALU.add).then_inc(S["mix_ready"], 1)
            then(pool.tensor_tensor(br_bc[:], br_bc[:], br_raw[:], ALU.add))
            pool.wait_ge(S["consts"], 1)
            pool.memset(fence[:], 0.0).then_inc(S["prep_done"], 1)

            for g in range(GROUPS):
                pool.wait_ge(S["dest_ready"], g + 1)
                for j in range(GROUP):
                    rows = TAIL if GROUP * g + j == TILES - 1 else P
                    for k in range(2):
                        pool.indirect_dma_start(
                            out=routed[:, :], out_offset=bass.IndirectOffsetOnAxis(dest[0:rows, g % RINGS, k, j:j + 1], 0),
                            in_=ring[g % RINGS][0:rows, j, :], in_offset=None).then_inc(sent[g % RINGS], 16)
            pool.wait_ge(S["prep_done"], 1)
            pool.memset(fence[:], 0.0).then_inc(S["carried"], 1)

            def send_y(s, q):
                pool.wait_ge(S["y_ready"], 2 * s + 2)
                if later(s, 1):
                    pool.wait_ge(S["y_sent"], 32 * s)
                pool.wait_ge(S["carried"], s + 1)
                pool.tensor_tensor(fence[:], fence[:], fence[:], ALU.add).then_inc(S["carried"], 1)
                for h in range(2):
                    pool.indirect_dma_start(out=out[:, :], out_offset=bass.IndirectOffsetOnAxis(y_row[:, q, h:h + 1], 0),
                                            in_=ybuf[:, q % 2, h, :], in_offset=None,
                                            compute_op=ALU.add).then_inc(S["y_sent"], 16)

            for t in (TILES - GROUP, TILES - 1):
                q, count = store_of(t)
                pool.wait_ge(x1_kept[q], count)
            pool.wait_ge(S["rows_zeroed"], 16)
            for q in range(4):
                send_y(q, q)
            with pool.Fori(1, SLOT_TILES // 4) as i:
                for q in range(4):
                    send_y(4 * i + q, q)

        @block.scalar
        def _(act):
            with act.Fori(0, E // 2) as i:
                for b in range(2):
                    act.wait_ge(stage_w2[b], 16 * i + 16)
                    act.copy(w2h[:, bass.ds((2 * i + b) * EW, EW)], stage[b]).then_inc(S["w2_high"], 1)
            act.wait_ge(S["small_in"], 32)
            act.wait_ge(S["gnn_in"], 16 * GNN_LOADS)
            for k in range(KD):
                act.activation(wr_g[:, k, :], wr_raw[:, k, :], ACT.Copy, scale=gb[:, 0, k:k + 1]).then_inc(S["wrg_ready"], 1)
            act.wait_ge(S["mix_ps"], 2)
            act.copy(mix[0:5, :], bank[2][0:5, 0:D]).then_inc(S["mix_copied"], 1)
            act.copy(br_bc[:], bank[3][:, 0:E]).then_inc(S["mix_copied"], 1)
            act.wait_ge(S["sqrt_in"], 1)
            act.activation(fw[:, 6, :], fw[:, 9, :], ACT.Sqrt).then_inc(S["sqrt_out"], 1)

            for slot in range(LAST_SLOT):
                if slot < TILES:
                    t = slot
                    act.wait_ge(S["hid_ps"], t + 1)
                    if t >= 2:
                        act.wait_ge(S["gnn_ps"], t - 1)
                    act.activation(g_t[:, t % 2, :, :], bank[4 + t % 2][:, 0:KD * P].rearrange("p (k n) -> p k n", k=KD),
                                   ACT.Relu).then_inc(S["hid_ready"], 1)
                g, rest = divmod(slot - (GROUP + 1), GROUP)
                if rest == 0 and 0 <= g < GROUPS:
                    act.wait_ge(S["var_ready"], g + 1)
                    act.activation(rt[:, 1, :], rt[:, 0, :], ACT.Sqrt).then_inc(S["std_ready"], 1)
                for t in u_tiles(slot):
                    act.wait_ge(S["ut_ps"], t + 1)
                    if t >= 2:
                        act.wait_ge(S["logit_ps"], t - 1)
                    act.copy(u_t[:, t % 2, :, :],
                             bank[2 + t % 2][:, 0:KD * P].rearrange("p (k n) -> p k n", k=KD)).then_inc(S["ut_ready"], 1)
                for t in u_tiles(slot + 1):
                    g, j = divmod(t, GROUP)
                    act.wait_ge(S["norm_ready"], g + 1)
                    q, count = store_of(t)
                    act.wait_ge(x1_kept[q], count)
                    act.activation(ring[g % RINGS][:, j, 0:D], ring[g % RINGS][:, j, 0:D], ACT.Identity,
                                   bias=nmean[:, g % RINGS, j:j + 1], scale=rstd[:, g % RINGS, j:j + 1]).then_inc(S["u_ready"], 1)

            def high_x(s, b):
                act.wait_ge(S["xt_ps"], s + 1)
                if later(s, 2):
                    act.wait_ge(S["h_ps"], KH * (s - 1))
                act.copy(xth[:, b, :, :], bank[b][:, :].rearrange("p (k n) -> p k n", k=KD)).then_inc(S["xth_ready"], 1)

            def tanh(s, b):
                act.wait_ge(S["meta_ready"], s + 1)
                if later(s, 2):
                    act.wait_ge(S["weight_ready"], s - 1)
                act.activation(half_tanh[:, b, :], lead[:, b, 1, :], ACT.Tanh, scale=0.5).then_inc(S["tanh_ready"], 1)

            def high_weights(s, b, e):
                if later(s, 2):
                    act.wait_ge(S["h_ps"], KH * (s - 1))
                for k in range(KD):
                    act.activation(w1cur[:, b, 0, k * H:(k + 1) * H], w1r[:, bass.ds(e * EW + k * H, H)], ACT.Copy,
                                   scale=gb[:, 0, k:k + 1]).then_inc(S["wcur_high"], 1)

            def gelu(s, b, m):
                act.wait_ge(S["h_ps"], KH * s + m // 2 * 2 + 2)
                if later(s, 2):
                    act.wait_ge(S["htl_ready"], 2 * (s - 1))
                act.activation(hbuf[:, b, m, :], bank[2 + 2 * b + m // 2][:, (m % 2) * TILE:(m % 2 + 1) * TILE], ACT.Gelu,
                               bias=b1cur[:, b, m:m + 1]).then_inc(S["h_ready"], 1)

            def scale_y(s, q):
                act.wait_ge(S["yb_ready"], s + 1)
                for h in range(2):
                    act.activation(ybuf[:, q % 2, h, :], ybuf[:, q % 2, h, :], ACT.Copy,
                                   scale=weight[:, q, h:h + 1]).then_inc(S["y_ready"], 1)

            def expert_step(s, q, last=False):
                b = q % 2
                if not last:
                    e = act.value_load(slot_ei[0:1, bass.ds(s + 1, 1)], min_val=0, max_val=E - 1)
                    high_weights(s + 1, 1 - b, e)
                for m in range(KH):
                    gelu(s, b, m)
                    if m == 1 and not last:
                        tanh(s + 1, 1 - b)
                if not last:
                    high_x(s + 1, 1 - b)
                if later(s, 1):
                    scale_y(s - 1, (q - 1) % 4)

            act.wait_ge(S["table_ready"], 1)
            act.wait_ge(S["w1_in"], 16 * KD)
            e = act.value_load(slot_ei[0:1, 0:1], min_val=0, max_val=E - 1)
            high_weights(0, 0, e)
            tanh(0, 0)
            high_x(0, 0)
            for q in range(4):
                expert_step(q, q)
            with act.Fori(1, SLOT_TILES // 4 - 1) as i:
                for q in range(4):
                    expert_step(4 * i + q, q)
            for q in range(4):
                expert_step(SLOT_TILES - 4 + q, q, last=q == 3)
            scale_y(SLOT_TILES - 1, 3)

        @block.vector
        def _(dve):
            steps = [0]

            def then(ins):
                steps[0] += 1
                ins.then_inc(S["dve_step"], 1)
                dve.wait_ge(S["dve_step"], steps[0])

            dve.wait_ge(S["dst_in"], 16)
            dve.tensor_scalar(hi_i[0:EP, :], dst_i[0:EP, :], 6, None, ALU.logical_shift_right).then_inc(S["dve_step"], 1)
            dve.tensor_scalar(lo_i[0:EP, :], dst_i[0:EP, :], LO - 1, None, ALU.bitwise_and).then_inc(S["dve_step"], 1)
            steps[0] += 2
            dve.wait_ge(S["dve_step"], 2)
            dve.tensor_copy(dst_hi[0:EP, :], hi_i[0:EP, :]).then_inc(S["dve_step"], 1)
            dve.tensor_copy(dst_lo[0:EP, :], lo_i[0:EP, :]).then_inc(S["dve_step"], 1)
            steps[0] += 2
            dve.wait_ge(S["dve_step"], 4)
            dve.wait_ge(S["numbers"], 2)

            def onehots(c, b):
                cols = bass.ds(c * OH_TILES, OH_TILES)
                dve.tensor_tensor(oh_hi[0:EP, b, :, :], dst_hi[0:EP, cols].unsqueeze(1).to_broadcast([EP, HI, OH_TILES]),
                                  num_hi[0:EP, :, :], ALU.is_equal)
                dve.tensor_tensor(oh_lo[0:EP, b, :, :], dst_lo[0:EP, cols].unsqueeze(1).to_broadcast([EP, LO, OH_TILES]),
                                  num_lo[0:EP, :, :], ALU.is_equal).then_inc(S["onehot"], 1)

            onehots(0, 0)
            onehots(1, 1)
            with dve.Fori(1, CHUNKS // 2) as i:
                for b in range(2):
                    dve.wait_ge(S["onehot_used"], 2 * i + b - 1)
                    onehots(2 * i + b, b)

            dve.wait_ge(S["degree"], 1)
            dve.wait_ge(S["gnn_in"], 16 * GNN_LOADS)
            then(dve.tensor_scalar(fw[:, 0, :], bank[0][0:HI, 0:LO], 1.0 / (N - 1), None, ALU.mult))
            dve.tensor_scalar(fw[:, 9, :], fw[:, 0, :], 1e-30, None, ALU.max).then_inc(S["sqrt_in"], 1)
            dve.tensor_scalar(fw[:, 7, :], fw[:, 0, :], 1e-8, None, ALU.add)
            then(dve.tensor_tensor(fw[:, 5, :], fw[:, 0, :], noise, ALU.mult))
            dve.scalar_tensor_tensor(fw[:, 1, :], fw[:, 5, :], 0.1, fw[:, 0, :], ALU.mult, ALU.add)
            dve.memset(fw[:, 4, :], 1.0)
            then(dve.reciprocal(fw[:, 2, :], fw[:, 7, :]))
            dve.wait_ge(S["sqrt_out"], 1)
            dve.reciprocal(fw[:, 10, :], fw[:, 6, :])
            then(dve.tensor_tensor(fw[:, 8, :], fw[:, 6, :], fw[:, 6, :], ALU.mult))
            then(dve.tensor_tensor(fw[:, 8, :], fw[:, 0, :], fw[:, 8, :], ALU.subtract))
            then(dve.tensor_tensor(fw[:, 8, :], fw[:, 8, :], fw[:, 10, :], ALU.mult))
            dve.scalar_tensor_tensor(fw[:, 3, :], fw[:, 8, :], 0.5, fw[:, 6, :], ALU.mult, ALU.add).then_inc(S["feats_ready"], 1)

            def norm(g):
                if g:
                    dve.wait_ge(S["norm_ready"], g)
                dve.wait_ge(S["stats_ready"], GROUP * (g + 1))
                for j in range(GROUP):
                    last = dve.bn_aggr(mv[:, j, :], stats[:, g % 2, j, :])
                then(last)
                dve.tensor_scalar(rt[:, 0, :], mv[:, :, 1], 1.0 + LN_EPS, LN_EPS * LN_EPS, ALU.mult, ALU.add).then_inc(S["var_ready"], 1)

            def refine(g):
                dve.wait_ge(S["std_ready"], g + 1)
                then(dve.reciprocal(rt[:, 2, :], rt[:, 1, :]))
                then(dve.tensor_tensor(rt[:, 3, :], rt[:, 2, :], rt[:, 2, :], ALU.mult))
                then(dve.tensor_tensor(rt[:, 3, :], rt[:, 3, :], rt[:, 0, :], ALU.mult))
                then(dve.tensor_scalar(rt[:, 3, :], rt[:, 3, :], -0.5, 1.5, ALU.mult, ALU.add))
                then(dve.tensor_tensor(rstd[:, g % RINGS, :], rt[:, 3, :], rt[:, 2, :], ALU.mult))
                dve.scalar_tensor_tensor(nmean[:, g % RINGS, :], mv[:, :, 0], -1.0, rstd[:, g % RINGS, :],
                                         ALU.mult, ALU.mult).then_inc(S["norm_ready"], 1)

            wide = [P, GROUP, E]
            rev_b = rev[:, :].unsqueeze(1).to_broadcast(wide)

            def best_of(of, best, rank, onehot):
                then(dve.tensor_reduce(best[:], of[:], AX_X, ALU.max))
                then(dve.tensor_tensor(eqm[:], of[:], best[:, :].unsqueeze(2).to_broadcast(wide), ALU.is_equal))
                then(dve.tensor_tensor(eqm[:], eqm[:], rev_b, ALU.mult))
                then(dve.tensor_reduce(rank[:], eqm[:], AX_X, ALU.max))
                then(dve.tensor_tensor(onehot[:], rev_b, rank[:, :].unsqueeze(2).to_broadcast(wide), ALU.is_equal))

            def route_first(g):
                dve.wait_ge(S["logit_ps"], GROUP * (g + 1))
                dve.tensor_tensor(lg[:], bank[0][:, 0:GROUP * E].rearrange("p (j e) -> p j e", e=E),
                                  br_bc[:, :].unsqueeze(1).to_broadcast(wide), ALU.add).then_inc(S["logits_read"], 1)
                dve.wait_ge(S["logits_read"], g + 1)
                best_of(lg, m1, r1, oh1)

            def route_second(g):
                then(dve.scalar_tensor_tensor(lg2[:], oh1[:], -3e38, lg[:], ALU.mult, ALU.add))
                best_of(lg2, m2, r2, oh2)

            def route_mask(g):
                if g == GROUPS - 1:
                    dve.tensor_scalar(oh1[:, GROUP - 1, :], oh1[:, GROUP - 1, :], valid[:], None, ALU.mult)
                    then(dve.tensor_scalar(oh2[:, GROUP - 1, :], oh2[:, GROUP - 1, :], valid[:], None, ALU.mult))
                dve.tensor_tensor(both[:, GROUP:2 * GROUP, :], oh1[:], oh2[:], ALU.add).then_inc(S["mask_ready"], 1)
                r = g % RINGS
                dve.tensor_copy(ring[r][:, :, D], node_id[:, g * GROUP:(g + 1) * GROUP])
                dve.tensor_scalar(ring[r][:, :, D + 1], r1[:], -1.0, float(E), ALU.mult, ALU.add)
                dve.tensor_tensor(ring[r][:, :, D + 2], m1[:], m2[:], ALU.subtract)

            def route_places(g):
                r = g % RINGS
                dve.wait_ge(S["pos_ps"], g + 1)
                then(dve.tensor_tensor(posE[:], bank[1][:, 0:GROUP * E].rearrange("p (j e) -> p j e", e=E),
                                       fill[:, :].unsqueeze(1).to_broadcast(wide), ALU.add))
                dve.tensor_tensor(oh1[:], oh1[:], posE[:], ALU.mult)
                then(dve.tensor_tensor(oh2[:], oh2[:], posE[:], ALU.mult))
                dve.tensor_tensor(fill[:], fill[:], bank[1][:, GROUP * E:(GROUP + 1) * E], ALU.add)
                dve.tensor_reduce(dest[:, r, 0, :], oh1[:], AX_X, ALU.add)
                dve.tensor_reduce(dest[:, r, 1, :], oh2[:], AX_X, ALU.add).then_inc(S["dest_ready"], 1)

            dve.wait_ge(S["prep_done"], 1)
            dve.tensor_scalar(valid[:], node_id[:, 0:1], float(TAIL), None, ALU.is_lt)
            ROUTING = ((ROUTE_SLOT, route_first), (ROUTE_SLOT + 1, route_second), (ROUTE_SLOT + 2, route_mask),
                       (PLACE_SLOT, route_places))
            for slot in range(1, LAST_SLOT + 1):
                if slot <= TILES:
                    t = slot - 1
                    g, j = divmod(t, GROUP)
                    if j == 0:
                        dve.wait_ge(x_in[g % RINGS], 16 if g < RINGS else 32 if g + 1 < GROUPS else 48)
                    dve.wait_ge(S["gnn_ps"], t + 1)
                    xr = ring[g % RINGS][:, j, 0:D]
                    dve.tensor_tensor(xr, xr, bank[6 + t % 2][:, 0:D], ALU.add).then_inc(S["x1_ready"], 1)
                    dve.wait_ge(S["x1_ready"], t + 1)
                    dve.bn_stats(stats[:, g % 2, j, :], xr).then_inc(S["stats_ready"], 1)
                for g in range(GROUPS):
                    if slot == GROUP * g + GROUP:
                        norm(g)
                    if slot == GROUP * g + GROUP + 1:
                        refine(g)
                    for at, part in ROUTING:
                        if slot == GROUP * g + at:
                            part(g)

            dve.wait_ge(S["dest_ready"], GROUPS)
            dve.tensor_copy(pad_at[:], fill[:]).then_inc(S["fill_ready"], 1)
            then(dve.tensor_tensor(jump[:], fill[:], regions[:], ALU.subtract))
            then(dve.tensor_scalar(cnt_i[:], jump[:], float(TILE - 1), None, ALU.add))
            dve.memset(cum[:], 0.0)
            then(dve.tensor_scalar(ntile_i[:], cnt_i[:], 8, None, ALU.logical_shift_right))
            then(dve.tensor_copy(ntile[:], ntile_i[:]))
            then(dve.tensor_copy(cum[:, 0, 4:4 + E], ntile[:]))
            for n, d in enumerate((1, 2, 4)):
                then(dve.tensor_tensor(cum[:, (n + 1) % 2, 4:4 + E], cum[:, n % 2, 4:4 + E],
                                       cum[:, n % 2, 4 - d:4 + E - d], ALU.add))
            then(dve.tensor_scalar(jump[:], ntile[:], -float(TILE), float(REGION), ALU.mult, ALU.add))
            table = [P, SLOT_TILES, E]
            then(dve.tensor_tensor(cmp_a, slot_no[:, :].unsqueeze(2).to_broadcast(table),
                                   cum[:, 1, 4:4 + E].unsqueeze(1).to_broadcast(table), ALU.is_ge))
            dve.tensor_reduce(slot_e[:], cmp_a, AX_X, ALU.add)
            then(dve.tensor_tensor(cmp_b, cmp_a, jump[:, :].unsqueeze(1).to_broadcast(table), ALU.mult))
            dve.tensor_scalar(slot_ei[:], slot_e[:], float(E - 1), None, ALU.min)
            then(dve.tensor_reduce(slot_f, cmp_b, AX_X, ALU.add))
            then(dve.scalar_tensor_tensor(slot_f, slot_no[:], float(TILE), slot_f, ALU.mult, ALU.add))
            dve.tensor_scalar(slot_row[:], slot_f, float(SPARE_AT), None, ALU.min).then_inc(S["table_ready"], 1)
            dve.wait_ge(S["b1_in"], 16 * KH)
            dve.wait_ge(S["beta_w1"], 1)
            dve.tensor_tensor(b1t[:], b1_raw[:], bank[4][:, 0:E * KH], ALU.add).then_inc(S["b1_ready"], 1)

            def meta(s, q, in_count):
                b = q % 2
                dve.wait_ge(xg_in[b], in_count)
                if later(s, 2):
                    dve.wait_ge(S["tanh_ready"], s - 1)
                e1, gap = xg[:, b, :, D + 1], xg[:, b, :, D + 2]
                dve.scalar_tensor_tensor(lead[:, b, 0, :], e1, slot_e[:, bass.ds(s, 1)], gap,
                                         ALU.is_equal, ALU.mult).then_inc(S["meta_step"], 1)
                if later(s, 4):
                    dve.wait_ge(S["y_sent"], 32 * (s - 3))
                dve.tensor_copy(y_row[:, q, :], xg[:, b, :, D])
                dve.wait_ge(S["meta_step"], s + 1)
                dve.scalar_tensor_tensor(lead[:, b, 1, :], lead[:, b, 0, :], 2.0, gap, ALU.mult, ALU.subtract).then_inc(S["meta_ready"], 1)

            def low_weights(s, b, e):
                if later(s, 2):
                    dve.wait_ge(S["h_ready"], KH * (s - 1))
                dve.tensor_copy(b1cur[:, b, :], b1t[:, bass.ds(e * KH, KH)])
                for k in range(KD):
                    dve.wait_ge(S["wcur_high"], KD * s + k + 1)
                    cols = slice(k * H, (k + 1) * H)
                    dve.scalar_tensor_tensor(w1cur[:, b, 1, cols], w1r[:, bass.ds(e * EW + k * H, H)], gb[:, 0, k:k + 1],
                                             w1cur[:, b, 0, cols].bitcast(F32), ALU.mult, ALU.subtract).then_inc(S["wcur_ready"], 1)

            def low_x(s, b):
                dve.wait_ge(S["xth_ready"], s + 1)
                dve.tensor_tensor(xtl[:, b, :, :], bank[b][:, :].rearrange("p (k n) -> p k n", k=KD),
                                  xth[:, b, :, :].bitcast(F32), ALU.subtract).then_inc(S["xt_ready"], 1)

            def split_h(s, b, half):
                m = slice(2 * half, 2 * half + 2)
                dve.wait_ge(S["h_ready"], KH * s + 2 * half + 2)
                if later(s, 2):
                    dve.wait_ge(S["y_ps"], 2 * (s - 1))
                dve.tensor_copy(hth[:, b, m, :], hbuf[:, b, m, :]).then_inc(S["hth_ready"], 1)
                dve.wait_ge(S["hth_ready"], 2 * s + half + 1)
                dve.tensor_tensor(htl[:, b, m, :], hbuf[:, b, m, :], hth[:, b, m, :].bitcast(F32),
                                  ALU.subtract).then_inc(S["htl_ready"], 1)

            def softmax(s, q):
                dve.wait_ge(S["tanh_ready"], s + 1)
                if later(s, 4):
                    dve.wait_ge(S["y_ready"], 2 * (s - 3))
                dve.tensor_scalar(weight[:, q, :], half_tanh[:, q % 2, :], 0.5, 0.5, ALU.mult, ALU.add).then_inc(S["weight_ready"], 1)

            def bias_y(s, q, e):
                dve.wait_ge(S["y_ps"], 2 * s + 2)
                dve.wait_ge(S["weight_ready"], s + 1)
                if later(s, 2):
                    dve.wait_ge(S["y_sent"], 32 * (s - 1))
                b = q % 2
                dve.tensor_tensor(ybuf[:, b, :, :], bank[6 + b][:, :].rearrange("p (h d) -> p h d", h=2),
                                  b2_bc[:, bass.ds(e * D, D)].unsqueeze(1).to_broadcast([P, 2, D]),
                                  ALU.add).then_inc(S["yb_ready"], 1)

            def expert_step(s, q, next_in, last=False):
                b = q % 2
                if not last:
                    e = dve.value_load(slot_ei[0:1, bass.ds(s + 1, 1)], min_val=0, max_val=E - 1)
                    meta(s + 1, (q + 1) % 4, next_in)
                    low_weights(s + 1, 1 - b, e)
                split_h(s, b, 0)
                if not last:
                    softmax(s + 1, (q + 1) % 4)
                    low_x(s + 1, 1 - b)
                split_h(s, b, 1)
                if later(s, 1):
                    e = dve.value_load(slot_ei[0:1, bass.ds(s - 1, 1)], min_val=0, max_val=E - 1)
                    bias_y(s - 1, (q - 1) % 4, e)

            dve.wait_ge(S["w1_in"], 16 * KD)
            dve.wait_ge(S["b1_ready"], 1)
            dve.wait_ge(S["table_ready"], 1)
            e = dve.value_load(slot_ei[0:1, 0:1], min_val=0, max_val=E - 1)
            low_weights(0, 0, e)
            meta(0, 0, 16)
            softmax(0, 0)
            low_x(0, 0)
            for r in range(RINGS):
                dve.wait_ge(sent[r], 32 * GROUP * len(range(r, GROUPS, RINGS)))
            dve.wait_ge(S["b2_in"], 16)
            for q in range(4):
                expert_step(q, q, 16 * ((q + 1) // 2 + 1))
            with dve.Fori(1, SLOT_TILES // 4 - 1) as i:
                for q in range(4):
                    expert_step(4 * i + q, q, 32 * i + 16 * ((q + 1) // 2 + 1))
            for q in range(4):
                s = SLOT_TILES - 4 + q
                expert_step(s, q, 16 * ((s + 1) // 2 + 1), last=q == 3)
            e = dve.value_load(slot_ei[0:1, SLOT_TILES - 1:SLOT_TILES], min_val=0, max_val=E - 1)
            bias_y(SLOT_TILES - 1, 3, e)

        @block.tensor
        def _(pe):
            pe.wait_ge(S["zeroed"], 1)
            zero_b = zeros.bitcast(BF16)
            pe.matmul(bank[0][0:HI, 0:LO], zero_b[0:EP, 0:HI], zero_b[0:EP, 0:LO], start=True, stop=False)
            with pe.Fori(0, CHUNKS // 2) as i:
                for b in range(2):
                    pe.wait_ge(S["onehot"], 2 * i + b + 1)
                    for t in range(OH_TILES):
                        mm = pe.matmul(bank[0][0:HI, 0:LO], oh_hi[0:EP, b, :, t], oh_lo[0:EP, b, :, t], start=False, stop=False)
                    mm.then_inc(S["onehot_used"], 1)
            pe.matmul(bank[0][0:HI, 0:LO], zero_b[0:EP, 0:HI], zero_b[0:EP, 0:LO], start=False, stop=True).then_inc(S["degree"], 1)
            pe.wait_ge(S["gnn_in"], 16 * GNN_LOADS)
            for k in range(KD):
                mm = pe.matmul(bank[2][0:5, 0:D], vec_w[:, k, :], w1g[:, k, :], start=(k == 0), stop=(k == KD - 1))
            mm.then_inc(S["mix_ps"], 1)
            pe.wait_ge(S["beta_bc_ready"], KD)
            for k in range(KD):
                mm = pe.matmul(bank[3][:, 0:E], beta_bc[:, k, :], wr_raw[:, k, :], start=(k == 0), stop=(k == KD - 1))
            mm.then_inc(S["mix_ps"], 1)

            def hidden(t):
                g, j = divmod(t, GROUP)
                if j == 0:
                    pe.wait_ge(feat_in[g % 2], 16 * (g // 2 + 1))
                if t >= 2:
                    pe.wait_ge(S["hid_ready"], t - 1)
                for k in range(KD):
                    mm = pe.matmul(bank[4 + t % 2][:, k * P:(k + 1) * P], mix[0:5, k * P:(k + 1) * P],
                                   feat[0:5, g % 2, j * P:(j + 1) * P], start=True, stop=True)
                mm.then_inc(S["hid_ps"], 1)

            def gnn_out(t):
                pe.wait_ge(S["hid_ready"], t + 1)
                if t >= 2:
                    pe.wait_ge(S["x1_ready"], t - 1)
                o = bank[6 + t % 2][:, 0:D]
                pe.matmul(o, three[:, :], b2g, start=True, stop=False)
                for k in range(KD):
                    mm = pe.matmul(o, g_t[:, t % 2, k, :], w2g[:, k, :], start=False, stop=(k == KD - 1))
                mm.then_inc(S["gnn_ps"], 1)

            def turn_u(t):
                g, j = divmod(t, GROUP)
                pe.wait_ge(S["u_ready"], t + 1)
                if t >= 2:
                    pe.wait_ge(S["ut_ready"], t - 1)
                for k in range(KD):
                    mm = pe.transpose(bank[2 + t % 2][:, k * P:(k + 1) * P], ring[g % RINGS][:, j, k * P:(k + 1) * P], ident[:, :])
                mm.then_inc(S["ut_ps"], 1)

            def logits(t):
                g, j = divmod(t, GROUP)
                pe.wait_ge(S["ut_ready"], t + 1)
                if j == 0 and g:
                    pe.wait_ge(S["logits_read"], g)
                for k in range(KD):
                    mm = pe.matmul(bank[0][:, j * E:(j + 1) * E], u_t[:, t % 2, k, :], wr_g[:, k, :],
                                   start=(k == 0), stop=(k == KD - 1))
                mm.then_inc(S["logit_ps"], 1)

            def places(g):
                pe.wait_ge(S["mask_ready"], g + 1)
                m = both[:, :, :].rearrange("p j e -> p (j e)")
                for d in range(GROUP + 1):
                    mm = pe.matmul(bank[1][:, 0:(GROUP + 1) * E], (ones if d else below)[:, :],
                                   m[:, (GROUP - d) * E:(2 * GROUP + 1 - d) * E], start=(d == 0), stop=(d == GROUP))
                mm.then_inc(S["pos_ps"], 1)

            pe.wait_ge(S["prep_done"], 1)
            pe.wait_ge(S["mix_ready"], 1)
            pe.wait_ge(S["wrg_ready"], KD)
            for slot in range(LAST_SLOT + 1):
                if slot < TILES:
                    hidden(slot)
                for t in u_tiles(slot):
                    turn_u(t)
                if 1 <= slot <= TILES:
                    gnn_out(slot - 1)
                for t in u_tiles(slot - 1):
                    logits(t)
                g, rest = divmod(slot - PLACE_SLOT, GROUP)
                if g >= 0 and rest == 0:
                    places(g)

            pe.wait_ge(S["hid_ready"], TILES)
            pe.wait_ge(S["w1_in"], 16 * KD)
            for e in range(E):
                for m in range(KH):
                    for k in range(KD):
                        at = e * EW + k * H + m * P
                        mm = pe.matmul(bank[4][:, e * KH + m:e * KH + m + 1], w1r[:, at:at + P], gb[:, 1, k:k + 1],
                                       start=(k == 0), stop=(k == KD - 1))
            mm.then_inc(S["beta_w1"], 1)

            def turn_x(s, b, in_count):
                pe.wait_ge(xg_in[b], in_count)
                if later(s, 2):
                    pe.wait_ge(S["xt_ready"], s - 1)
                for h in range(2):
                    for k in range(KD):
                        mm = pe.transpose(bank[b][:, k * TILE + h * P:k * TILE + (h + 1) * P],
                                          xg[:, b, h, k * P:(k + 1) * P], ident[:, :])
                mm.then_inc(S["xt_ps"], 1)

            def layer1(s, b):
                pe.wait_ge(S["xt_ready"], s + 1)
                pe.wait_ge(S["wcur_ready"], 2 * s + 2)
                if later(s, 2):
                    pe.wait_ge(S["h_ready"], KH * (s - 1))
                for m in range(KH):
                    o = bank[2 + 2 * b + m // 2][:, (m % 2) * TILE:(m % 2 + 1) * TILE]
                    for k in range(KD):
                        cols = slice(k * H + m * P, k * H + (m + 1) * P)
                        pe.matmul(o, w1cur[:, b, 0, cols], xth[:, b, k, :], start=(k == 0), stop=False)
                        pe.matmul(o, w1cur[:, b, 0, cols], xtl[:, b, k, :], start=False, stop=False)
                        mm = pe.matmul(o, w1cur[:, b, 1, cols], xth[:, b, k, :], start=False, stop=(k == KD - 1))
                    mm.then_inc(S["h_ps"], 1)

            def layer2(s, b):
                e = pe.value_load(slot_ei[0:1, bass.ds(s, 1)], min_val=0, max_val=E - 1)
                pe.wait_ge(S["htl_ready"], 2 * s + 2)
                if later(s, 2):
                    pe.wait_ge(S["yb_ready"], s - 1)
                for h in range(2):
                    o = bank[6 + b][:, h * D:(h + 1) * D]
                    tok = slice(h * P, (h + 1) * P)
                    for k in range(KH):
                        high = w2h[:, bass.ds(e * EW + k * D, D)]
                        low = w2l[:, bass.ds(e * EW + k * D, D)]
                        pe.matmul(o, hth[:, b, k, tok], high, start=(k == 0), stop=False)
                        pe.matmul(o, hth[:, b, k, tok], low, start=False, stop=False)
                        mm = pe.matmul(o, htl[:, b, k, tok], high, start=False, stop=(k == KH - 1))
                    mm.then_inc(S["y_ps"], 1)

            def expert_step(s, q, next_in, last=False):
                b = q % 2
                layer1(s, b)
                if not last:
                    turn_x(s + 1, 1 - b, next_in)
                if later(s, 1):
                    layer2(s - 1, 1 - b)

            pe.wait_ge(S["table_ready"], 1)
            pe.wait_ge(S["b1_ready"], 1)
            turn_x(0, 0, 16)
            for q in range(2):
                expert_step(q, q, 16 * ((q + 1) // 2 + 1))
            with pe.Fori(1, SLOT_TILES // 2 - 1) as i:
                for q in range(2):
                    expert_step(2 * i + q, q, 16 * i + 16 * ((q + 1) // 2 + 1))
            for q in range(2):
                s = SLOT_TILES - 2 + q
                expert_step(s, q, 16 * ((s + 1) // 2 + 1), last=q == 1)
            layer2(SLOT_TILES - 1, 1)


_INS = ["x", "dst", "node_vec", "L0_gnn_W_deg", "L0_gnn_b_deg", "L0_gnn_W_bet", "L0_gnn_b_bet", "L0_gnn_W_clo",
        "L0_gnn_b_clo", "L0_gnn_W_eig", "L0_gnn_b_eig", "L0_gnn_W1", "L0_gnn_b1", "L0_gnn_W2", "L0_gnn_b2",
        "L0_ffn_gamma", "L0_ffn_beta", "L0_ffn_Wr", "L0_ffn_br", "L0_ffn_W1", "L0_ffn_b1", "L0_ffn_W2", "L0_ffn_b2"]


def kernel(**inputs):
    import numpy as _np
    import concourse.bacc as _bacc
    from concourse import mybir as _mybir
    from concourse.bass_utils import run_bass_kernel_spmd as _run

    nc = _bacc.Bacc("TRN2", target_bir_lowering=False, num_devices=1)
    arrays, args = {}, []
    for name in _INS:
        a = _np.ascontiguousarray(inputs[name])
        arrays[f"in_{name}_dram"] = a
        args.append(nc.dram_tensor(f"in_{name}_dram", a.shape, _mybir.dt.from_np(a.dtype), kind="ExternalInput").ap())
    n, d = inputs["x"].shape
    args.append(nc.dram_tensor("out_0_dram", (n + TILE, d), _mybir.dt.float32, kind="ExternalOutput").ap())
    gnn_ffn_kernel(nc, *args)
    r = _run(nc, [arrays], core_ids=[0])
    return r.results[0]["out_0_dram"][:n]
```

```python
from contextlib import ExitStack

import concourse.bass as bass
from concourse import mybir

ALU = mybir.AluOpType
ACT = mybir.ActivationFunctionType
AX_X = mybir.AxisListType.X
F32 = mybir.dt.float32
F32R = mybir.dt.float32r
BF16 = mybir.dt.bfloat16
I32 = mybir.dt.int32
U32 = mybir.dt.uint32

P = 128
LN_EPS = 1e-5

LO = 64
OH_TILES = 16

GROUP = 7
RINGS = 5

TILE = 256

U_SLOT = 10
ROUTE_SLOT = 16
PLACE_SLOT = 19

GNN_LOADS = 15

SIGNALS = """
    dst_in small_in gnn_in zeroed numbers consts prep_done spare_sent bias_moved rows_zeroed
    beta_bc_ready w1_in b1_in b2_in mix_ps mix_copied mix_split mix_placed wrg_ready
    w2_high w2_low onehot onehot_used degree sqrt_in sqrt_out feats_ready feat_kept
    pool_step dve_step
    hid_ps hid_ready gnn_ps x1_ready stats_ready var_ready std_ready norm_ready
    u_ready ut_ps ut_ready logit_ps logits_read mask_ready pos_ps dest_ready fill_ready early_table late_table
    pads_sent wcur_high wcur_low0 wcur_low1
    xt_ps xn_ready xth_ready xt_ready lead_step lead_ready tanh_ready weight_ready h_ps h_ready hth_first hth_second htl_ready
    y_ps yb_ready y_ready y_sent carried
""".split()


def later(s, d):
    return not isinstance(s, int) or s >= d


def gnn_ffn_kernel(nc, x, dst, node_vec, g_wdeg, g_bdeg, g_wbet, g_bbet, g_wclo, g_bclo, g_weig, g_beig,
                   g_w1, g_b1, g_w2, g_b2, gamma, beta, wr, br, w1, b1, w2, b2, out):
    N, D = x.shape
    E, _, H = w1.shape
    n_edges = dst.shape[0]
    KD, KH = D // P, H // P
    EW = KD * H
    TILES = -(-N // P)
    TAIL = N - (TILES - 1) * P
    GROUPS = TILES // GROUP
    assert GROUPS * GROUP == TILES and RINGS < GROUPS <= RINGS + 2 and D == 256 and H == 512 and E == 8
    assert KH * D == EW
    NPAD = TILES * P
    HI = NPAD // LO
    EP = 125
    ECOLS = n_edges // EP
    CHUNKS = ECOLS // OH_TILES
    assert EP * ECOLS == n_edges and CHUNKS * OH_TILES == ECOLS and CHUNKS == 6 * E + 2
    REGION = NPAD + TILE
    ROW = D + 3
    SLOT_TILES = (2 * N + E * (TILE - 1)) // TILE
    SPARE_AT = E * REGION
    EARLY_GROUPS = GROUPS - 3
    EARLY = (2 * EARLY_GROUPS * GROUP * P - E * (TILE - 1)) // TILE // 2 * 2
    assert SLOT_TILES % 8 == 0 and EARLY_GROUPS == RINGS - 1 and EARLY >= 4 + E

    with ExitStack() as ctx:
        def sb(name, shape, dt):
            return ctx.enter_context(nc.sbuf_tensor(name, shape, dt))

        def sem(name):
            return ctx.enter_context(nc.semaphore(name))

        ctx.enter_context(nc.allow_low_precision(reason="sums of row numbers are exact integers in float32"))
        ctx.enter_context(nc.allow_non_contiguous_dma(reason="a few short vectors are laid over partitions"))

        feat_dram = nc.dram_tensor("feat_dram", (3 * 5, NPAD), BF16).ap()
        routed = nc.dram_tensor("routed", (SPARE_AT + TILE, ROW), F32).ap()

        w1r = sb("w1r", [P, E * EW], F32)
        w2h = sb("w2h", [P, E * EW], F32R)
        w2l = sb("w2l", [P, E * EW], F32R)
        b1t = sb("b1t", [P, E * KH], F32)
        three = sb("three", [P, P], BF16)
        ident = sb("ident", [P, P], F32)
        below = sb("below", [P, P], BF16)
        ones = sb("ones", [P, P], BF16)
        wr_g = sb("wr_g", [P, KD, E], F32)
        br_bc = sb("br_bc", [P, E], F32)
        br_raw = sb("br_raw", [P, E], F32)
        rev = sb("rev", [P, E], F32)
        node_id = sb("node_id", [P, TILES], F32)
        fill = sb("fill", [P, E], F32)
        regions = sb("regions", [P, E], F32)
        slot_no = sb("slot_no", [P, SLOT_TILES], F32)
        slot_e = sb("slot_e", [P, SLOT_TILES], F32)
        slot_ei = sb("slot_ei", [P, SLOT_TILES], I32)
        slot_row = sb("slot_row", [P, SLOT_TILES], I32)
        pad_rows = sb("pad_rows", [P, 2, ROW], F32)
        zeros = pad_rows[:, 0, 0:D]
        fence = sb("fence", [P, 1], F32)

        xg = sb("xg", [P, 2, 2, ROW], F32)
        xth = sb("xth", [P, 2, KD, TILE], F32R)
        xtl = sb("xtl", [P, 2, KD, TILE], F32R)
        hbuf = sb("hbuf", [P, 2, KH, TILE], F32)
        hth = sb("hth", [P, 2, KH, TILE], F32R)
        htl = sb("htl", [P, 2, KH, TILE], F32R)
        w1cur = sb("w1cur", [P, 2, 2, EW], F32R)
        b1cur = sb("b1cur", [P, 2, KH], F32)
        y_row = sb("y_row", [P, 4, 2], U32)
        lead = sb("lead", [P, 2, 2, 2], F32)
        half_tanh = sb("half_tanh", [P, 2, 2], F32)
        weight = sb("weight", [P, 4, 2], F32)
        stage = [hbuf[:, b, :, :].rearrange("p k n -> p (k n)") for b in range(2)]

        gb = sb("gb", [P, 2, KD], F32)
        stats = sb("stats", [P, 2, GROUP, 6], F32)
        mv = sb("mv", [P, GROUP, 2], F32)
        rt = sb("rt", [P, 4, GROUP], F32)
        rstd = sb("rstd", [P, RINGS, GROUP], F32)
        nmean = sb("nmean", [P, RINGS, GROUP], F32)
        lg = sb("lg", [P, GROUP, E], F32)
        lg2 = sb("lg2", [P, GROUP, E], F32)
        eqm = sb("eqm", [P, GROUP, E], F32)
        oh1 = sb("oh1", [P, GROUP, E], F32)
        oh2 = sb("oh2", [P, GROUP, E], F32)
        both = sb("both", [P, 2 * GROUP + 1, E], BF16)
        posE = sb("posE", [P, GROUP, E], F32)
        m1 = sb("m1", [P, GROUP], F32)
        m2 = sb("m2", [P, GROUP], F32)
        r1 = sb("r1", [P, GROUP], F32)
        r2 = sb("r2", [P, GROUP], F32)
        start = sb("start", [P, 1], F32)
        valid = sb("valid", [P, 1], F32)
        dest = sb("dest", [P, RINGS, 2, GROUP], U32)
        pad_at = sb("pad_at", [P, E], I32)
        cnt_i = sb("cnt_i", [P, E], I32)
        ntile_i = sb("ntile_i", [P, E], I32)
        ntile = sb("ntile", [P, E], F32)
        cum = sb("cum", [P, 2, 4 + E], F32)
        jump = sb("jump", [P, E], F32)
        early_fill = sb("early_fill", [P, E], F32)
        early = sb("early", [P, E + 1], F32)

        ARENA = 13184
        arena = sb("arena", [P, ARENA], F32)

        def view(at, words):
            assert at + words <= ARENA
            return arena[:, at:at + words]

        RW = GROUP * ROW
        ring = [view(r * RW, RW).rearrange("p (j r) -> p j r", r=ROW) for r in range(RINGS)]
        at_feat = RINGS * RW
        at_ut = at_feat + 2 * GROUP * P
        at_gt = at_ut + 2 * D
        at_w2g = at_gt + 2 * D
        at_mix = at_w2g + KD * D
        at_small = at_mix + D
        FROWS = 6 * 5
        feat = view(at_feat, GROUP * P).bitcast(BF16).rearrange("p (b n) -> p b n", b=2)[0:FROWS, :, :]
        u_t = view(at_ut, 2 * D).rearrange("p (b k n) -> p b k n", b=2, k=KD)
        g_t = view(at_gt, 2 * D).rearrange("p (b k n) -> p b k n", b=2, k=KD)
        w2g = view(at_w2g, KD * D).rearrange("p (k d) -> p k d", k=KD)
        mix = view(at_mix, D)[0:5, :]
        b2g = view(at_small, D // 2).bitcast(BF16)
        noise = view(at_small + D // 2, LO)[0:HI, :]
        wr_raw = view(at_small + D // 2 + LO, KD * E).rearrange("p (k e) -> p k e", k=KD)
        vec_w = view(at_small + D // 2 + LO + KD * E, KD * 5).rearrange("p (k q) -> p k q", k=KD)
        beta_bc = view(at_small + D // 2 + LO + KD * E + KD * 5, KD * P).rearrange("p (k m) -> p k m", k=KD)
        w1g = view(at_ut, KD * D).rearrange("p (k d) -> p k d", k=KD)
        fw = view(at_feat, 12 * LO)[0:HI, :].rearrange("p (f l) -> p f l", f=12)
        fparts = view(at_feat + 12 * LO, 15 * LO // 2).bitcast(BF16).rearrange("p (q f l) -> p q f l", q=3, f=5)[0:HI, :, :, :]
        frest = view(at_feat + 12 * LO + 15 * LO // 2, 5 * LO).rearrange("p (f l) -> p f l", f=5)[0:HI, :, :]
        at_mixparts = at_feat + 12 * LO + 15 * LO // 2 + 5 * LO
        assert GROUP * P <= at_mixparts - at_feat and at_mixparts + D // 2 <= at_ut
        mix_rows = view(at_mixparts, D // 2).bitcast(BF16)[0:FROWS, :]
        mix_parts = view(at_ut, 3 * D // 2).bitcast(BF16).rearrange("p (q n) -> p q n", q=3)[0:5, :, :]
        bias_f = view(at_feat + 12 * LO, D)[0:1, :]
        bias_p = view(at_feat + 12 * LO + D, 3 * D // 2).bitcast(BF16).rearrange("p (q n) -> p q n", q=3)[0:1, :, :]
        mix_bias = xg[0:5, 0, 0, 0:D]
        used = [RW]

        def hist(words):
            used[0] += words
            assert used[0] <= at_feat + 12 * LO
            return view(used[0] - words, words)

        oh_hi = hist(4 * HI * OH_TILES // 2).bitcast(BF16).rearrange("p (b j t) -> p b j t", b=4, t=OH_TILES)
        at_dst = used[0]
        oh_lo = hist(4 * LO * OH_TILES // 2).bitcast(BF16).rearrange("p (b j t) -> p b j t", b=4, t=OH_TILES)
        num_hi = hist(HI * OH_TILES // 2).bitcast(BF16).rearrange("p (j t) -> p j t", t=OH_TILES)
        num_lo = hist(LO * OH_TILES // 2).bitcast(BF16).rearrange("p (j t) -> p j t", t=OH_TILES)
        dst_hi = hist(ECOLS // 2).bitcast(BF16)
        dst_lo = hist(ECOLS // 2).bitcast(BF16)
        dst_i = view(at_dst, ECOLS).bitcast(I32)
        lo_i = view(at_dst + ECOLS, ECOLS).bitcast(I32)
        hi_i = view(at_dst - ECOLS, ECOLS).bitcast(I32)
        at_b2 = 3 * RW
        at_cmp = at_gt
        assert at_b2 + E * D + 4 * D <= RINGS * RW
        ybuf = view(at_b2 + E * D, 4 * D).rearrange("p (b h d) -> p b h d", b=2, h=2)
        xn = view(2 * RW, 2 * KD * TILE).rearrange("p (b k n) -> p b k n", b=2, k=KD)
        b2_bc = view(at_b2, E * D)
        cmp_a = view(at_cmp, SLOT_TILES * E).rearrange("p (s e) -> p s e", e=E)
        cmp_b = view(at_cmp + SLOT_TILES * E, SLOT_TILES * E).rearrange("p (s e) -> p s e", e=E)
        slot_f = view(at_cmp + 2 * SLOT_TILES * E, SLOT_TILES)

        bank = [ctx.enter_context(nc.psum_tensor(f"bank{i}", [P, 512], F32)) for i in range(8)]

        S = {}
        for name in SIGNALS:
            S[name] = sem("s_" + name)
        x_in = [sem(f"s_x_in{r}") for r in range(RINGS)]
        feat_in = [sem(f"s_feat_in{r}") for r in range(2)]
        x1_kept = [sem(f"s_x1_kept{q}") for q in range(4)]
        sent = [sem(f"s_sent{r}") for r in range(RINGS)]
        stage_w2 = [sem(f"s_stage_w2_{b}") for b in range(2)]
        xg_in = [sem(f"s_xg_in{r}") for r in range(2)]

        block = ctx.enter_context(nc.Block())

        w2_dram = w2.rearrange("e (k p) d -> e p k d", p=P)

        def node_parts(dram, first, count):
            whole = count if first + count < TILES else count - 1
            parts = [(P, slice(0, whole), dram[first * P:(first + whole) * P, :].rearrange("(j p) d -> p j d", p=P))]
            if whole < count:
                parts.append((TAIL, whole, dram[(first + whole) * P:N, :]))
            return parts

        FIRST_PART = 4

        def store_of(t):
            g, j = divmod(t, GROUP)
            count = 16 * (g // 2 + 1)
            return (2 * (g % 2), count) if j < FIRST_PART else (2 * (g % 2) + 1, count if g + 1 < GROUPS else count + 16)

        LAST_STORES = (TILES - 2 * GROUP, TILES - GROUP - 1, TILES - GROUP, TILES - 1)

        def u_tiles(slot):
            found = []
            for g in range(GROUPS):
                n = slot - GROUP * g - U_SLOT
                if 0 <= n < (GROUP + 1) // 2:
                    found += [GROUP * g + j for j in (2 * n, 2 * n + 1) if j < GROUP]
            return found

        LAST_SLOT = GROUP * (GROUPS - 1) + PLACE_SLOT

        @block.sync
        def _(sp):
            sp.dma_start(dst_i[0:EP, :], dst.rearrange("(p c) -> p c", c=ECOLS)).then_inc(S["dst_in"], 16)
            sp.dma_start(gb[:, 0, :], gamma.rearrange("(k p) -> p k", p=P)).then_inc(S["small_in"], 16)
            sp.dma_start(gb[:, 1, :], beta.rearrange("(k p) -> p k", p=P)).then_inc(S["small_in"], 16)
            for k in range(KD):
                sp.dma_start(w1r[:, :].rearrange("p (e k h) -> p e k h", e=E, k=KD)[:, :, k, :],
                             w1[:, k * P:(k + 1) * P, :].rearrange("e p h -> p e h")).then_inc(S["w1_in"], 16)
            for b in range(2):
                sp.dma_start(stage[b].rearrange("p (k d) -> p k d", k=KH), w2_dram[b]).then_inc(stage_w2[b], 16)
            sp.dma_start(wr_raw, wr.rearrange("(k p) e -> p k e", p=P)).then_inc(S["gnn_in"], 16)
            sp.dma_start(w1g, g_w1.rearrange("(k p) h -> p k h", p=P)).then_inc(S["gnn_in"], 16)
            sp.dma_start(w2g, g_w2.rearrange("(k p) h -> p k h", p=P)).then_inc(S["gnn_in"], 16)
            sp.wait_ge(S["zeroed"], 1)
            for q, (wv, bv) in enumerate([(g_wdeg, g_bdeg), (g_wbet, g_bbet), (g_wclo, g_bclo), (g_weig, g_beig)]):
                rows = slice(64 * (q % 2), 64 * (q % 2) + 64)
                sp.dma_start(vec_w[rows, q // 2, q:q + 1], wv.rearrange("(p a) -> p a", a=1)).then_inc(S["gnn_in"], 16)
                sp.dma_start(vec_w[rows, q // 2, 4:5], bv.rearrange("(p a) -> p a", a=1)).then_inc(S["gnn_in"], 16)
            sp.dma_start(mix_bias[4:5, :], g_b1.rearrange("(a d) -> a d", a=1)).then_inc(S["gnn_in"], 16)
            sp.dma_start(noise[0:HI - 1, :], node_vec[0:(HI - 1) * LO].rearrange("(h l) -> h l", l=LO)).then_inc(S["gnn_in"], 16)
            sp.dma_start(noise[HI - 1:HI, 0:N - (HI - 1) * LO],
                         node_vec[(HI - 1) * LO:N].rearrange("(a l) -> a l", a=1)).then_inc(S["gnn_in"], 16)
            sp.dma_start(br_raw[:], br.rearrange("(a e) -> a e", a=1).to_broadcast([P, E])).then_inc(S["gnn_in"], 16)
            for m in range(KH):
                sp.dma_start(b1t[:, :].rearrange("p (e m) -> p e m", m=KH)[:, :, m],
                             b1.rearrange("e (m p) -> m p e", p=P)[m]).then_inc(S["b1_in"], 16)
            sp.dma_start(out[N:N + TILE, :].rearrange("(p h) d -> p h d", h=2), pad_rows[:, :, 0:D]).then_inc(S["rows_zeroed"], 16)
            sp.dma_start(routed[SPARE_AT:SPARE_AT + TILE, :].rearrange("(p h) r -> p h r", h=2), pad_rows[:]).then_inc(S["spare_sent"], 16)

            def load_x(g):
                for rows, j, part in node_parts(x, GROUP * g, GROUP):
                    sp.dma_start(ring[g % RINGS][0:rows, j, 0:D], part).then_inc(x_in[g % RINGS], 16)

            def load_features(g):
                at = 0
                for rows in (15, 10, 5):
                    sp.dma_start(feat[at:at + rows, g % 2, :],
                                 feat_dram[0:rows, g * GROUP * P:(g + 1) * GROUP * P]).then_inc(feat_in[g % 2], 16)
                    at += rows

            load_x(0)
            with sp.Fori(1, E // 2) as i:
                for b in range(2):
                    sp.wait_ge(S["w2_low"], 2 * i + b - 1)
                    sp.dma_start(stage[b].rearrange("p (k d) -> p k d", k=KH),
                                 w2_dram[bass.ds(2 * i + b, 1)].rearrange("a p k d -> p (a k) d")).then_inc(stage_w2[b], 16)

            sp.wait_ge(S["mix_split"], 1)
            for n, q in enumerate((0, 0, 0, 1, 1, 2)):
                sp.dma_start(mix_rows[5 * n:5 * n + 5, :], mix_parts[:, q, :]).then_inc(S["mix_placed"], 16)
            sp.wait_ge(S["feats_ready"], 1)
            sp.dma_start(feat_dram.rearrange("r (h l) -> h r l", l=LO),
                         fparts[:, :, :, :].rearrange("p q f l -> p (q f) l")).then_inc(S["feat_kept"], 16)
            load_x(1)
            sp.wait_ge(S["feat_kept"], 16)
            sp.wait_ge(S["prep_done"], 1)
            load_features(0)
            load_features(1)
            for g in range(2, RINGS):
                load_x(g)
            for g in range(GROUPS):
                for q, (first, count) in enumerate(((0, FIRST_PART), (FIRST_PART, GROUP - FIRST_PART))):
                    sp.wait_ge(S["x1_ready"], GROUP * g + first + count)
                    for rows, j, part in node_parts(out[0:N, :], GROUP * g + first, count):
                        src = ring[g % RINGS][0:rows, first + j, 0:D] if isinstance(j, int) else \
                            ring[g % RINGS][0:rows, first + j.start:first + j.stop, 0:D]
                        sp.dma_start(part, src).then_inc(x1_kept[2 * (g % 2) + q], 16)
                if g + 2 < GROUPS:
                    sp.wait_ge(S["hid_ps"], GROUP * (g + 1))
                    load_features(g + 2)
                if g >= 3 and g + 2 < GROUPS:
                    sp.wait_ge(sent[g - 3], 32 * GROUP)
                    load_x(g + 2)

            def load_slot(s, b):
                row = sp.value_load(slot_row[0:1, bass.ds(s, 1)], min_val=0, max_val=SPARE_AT)
                sp.dma_start(xg[:, b, :, :], routed[bass.ds(row, TILE), :].rearrange("(p h) r -> p h r", h=2)).then_inc(xg_in[b], 16)

            def load_slots(first, end):
                with sp.Fori(first, end) as i:
                    for b in range(2):
                        sp.wait_ge(S["weight_ready"], 2 * i + b - 1)
                        sp.wait_ge(S["xt_ps"], 2 * i + b - 1)
                        load_slot(2 * i + b, b)

            sp.wait_ge(S["early_table"], 1)
            for g in range(EARLY_GROUPS):
                sp.wait_ge(sent[g], 32 * GROUP)
            load_slot(0, 0)
            load_slot(1, 1)
            sp.wait_ge(sent[4], 32 * GROUP)
            sp.dma_start(b2_bc, b2.rearrange("e d -> (e d)").rearrange("(a n) -> a n", a=1).to_broadcast([P, E * D])).then_inc(S["b2_in"], 16)
            sp.wait_ge(S["fill_ready"], 1)
            for e in range(E):
                s, b = e + 2, e % 2
                sp.wait_ge(S["weight_ready"], s - 1)
                sp.wait_ge(S["xt_ps"], s - 1)
                load_slot(s, b)
                row = sp.value_load(pad_at[0:1, e:e + 1], min_val=0, max_val=SPARE_AT - TILE)
                sp.dma_start(routed[bass.ds(row, TILE), :].rearrange("(p h) r -> p h r", h=2), pad_rows[:]).then_inc(S["pads_sent"], 16)
            load_slots(1 + E // 2, EARLY // 2)
            sp.wait_ge(S["late_table"], 1)
            for g in range(GROUPS - 2, GROUPS):
                sp.wait_ge(sent[g % RINGS], 64 * GROUP)
            sp.wait_ge(S["pads_sent"], 16 * E)
            sp.wait_ge(S["spare_sent"], 16)
            load_slots(EARLY // 2, SLOT_TILES // 2)
            sp.wait_ge(S["y_sent"], 32 * SLOT_TILES)
            for t in LAST_STORES:
                q, count = store_of(t)
                sp.wait_ge(x1_kept[q], count)
            sp.wait_ge(S["rows_zeroed"], 16)

        @block.gpsimd
        def _(pool):
            steps = [0]

            def then(ins):
                steps[0] += 1
                ins.then_inc(S["pool_step"], 1)
                pool.wait_ge(S["pool_step"], steps[0])

            for q, (t, n) in enumerate([(num_hi, HI), (num_lo, LO)]):
                pool.iota(t, pattern=[[1, n], [0, OH_TILES]], base=0, channel_multiplier=0,
                          allow_small_or_imprecise_dtypes=True).then_inc(S["numbers"], 1)
            then(pool.memset(vec_w, 0.0))
            then(pool.memset(mix_bias, 0.0))
            then(pool.memset(noise, 0.0))
            then(pool.memset(pad_rows[:], 0.0))
            then(pool.iota(pad_rows[:, :, D], pattern=[[1, 2]], base=N, channel_multiplier=2,
                           allow_small_or_imprecise_dtypes=True))
            then(pool.memset(pad_rows[:, :, D + 1], -1.0))
            pool.memset(fence[:], 0.0).then_inc(S["zeroed"], 1)
            pool.wait_ge(S["small_in"], 32)
            for k in range(KD):
                pool.tensor_copy(beta_bc[:, k, :], gb[:, 1, k:k + 1].to_broadcast([P, P])).then_inc(S["beta_bc_ready"], 1)

            with pool.Fori(0, E // 2) as i:
                for b in range(2):
                    e = 2 * i + b
                    pool.wait_ge(S["w2_high"], e + 1)
                    at = bass.ds(e * EW, EW)
                    pool.tensor_tensor(w2l[:, at], stage[b], w2h[:, at].bitcast(F32), ALU.subtract).then_inc(S["w2_low"], 1)

            then(pool.memset(ident[:], 0.0))
            then(pool.affine_select(out=ident[:], in_=ident[:], compare_op=ALU.not_equal, fill=1.0, base=0,
                                    pattern=[[-1, P]], channel_multiplier=1))
            then(pool.memset(ones[:], 1.0))
            then(pool.affine_select(out=below[:], in_=ones[:], compare_op=ALU.is_gt, fill=0.0, base=0,
                                    pattern=[[1, P]], channel_multiplier=-1))
            then(pool.memset(three[:], 0.0))
            for part in range(3):
                then(pool.affine_select(out=three[:], in_=three[:], compare_op=ALU.not_equal, fill=1.0, base=-32 * part,
                                        pattern=[[0, P]], channel_multiplier=1))
            for t, step, n, base, per_row in ((rev, -1, E, E, 0), (fill, REGION, E, 0, 0), (regions, REGION, E, 0, 0),
                                              (node_id, P, TILES, 0, 1), (slot_no, 1, SLOT_TILES, 0, 0)):
                then(pool.iota(t[:], pattern=[[step, n]], base=base, channel_multiplier=per_row,
                               allow_small_or_imprecise_dtypes=True))
            then(pool.memset(both[:], 0.0))
            then(pool.memset(b2g, 0.0))
            pool.dma_start(bias_f, g_b2.rearrange("(a d) -> a d", a=1)).then_inc(S["bias_moved"], 16)
            pool.wait_ge(S["bias_moved"], 16)
            then(pool.tensor_copy(bias_p[:, 0, :], bias_f))
            for q in range(2):
                then(pool.tensor_tensor(bias_f, bias_f, bias_p[:, q, :], ALU.subtract))
                then(pool.tensor_copy(bias_p[:, q + 1, :], bias_f))
            for q in range(3):
                pool.dma_start(b2g[32 * q:32 * q + 1, :], bias_p[:, q, :]).then_inc(S["bias_moved"], 16)
            pool.wait_ge(S["bias_moved"], 64)
            pool.memset(fence[:], 0.0).then_inc(S["consts"], 1)
            pool.wait_ge(S["mix_copied"], 2)
            then(pool.tensor_tensor(mix, mix, mix_bias, ALU.add))
            then(pool.tensor_copy(mix_parts[:, 0, :], mix))
            for q in range(2):
                then(pool.tensor_tensor(mix, mix, mix_parts[:, q, :], ALU.subtract))
                then(pool.tensor_copy(mix_parts[:, q + 1, :], mix))
            pool.memset(fence[:], 0.0).then_inc(S["mix_split"], 1)
            then(pool.tensor_tensor(br_bc[:], br_bc[:], br_raw[:], ALU.add))
            pool.wait_ge(S["consts"], 1)
            pool.memset(fence[:], 0.0).then_inc(S["prep_done"], 1)

            pool.wait_ge(S["prep_done"], 1)
            pool.memset(fence[:], 0.0).then_inc(S["carried"], 1)

            def scatter(g, first=0, end=GROUP):
                pool.wait_ge(S["dest_ready"], g + 1)
                for j in range(first, end):
                    rows = TAIL if GROUP * g + j == TILES - 1 else P
                    for k in range(2):
                        pool.indirect_dma_start(
                            out=routed[:, :], out_offset=bass.IndirectOffsetOnAxis(dest[0:rows, g % RINGS, k, j:j + 1], 0),
                            in_=ring[g % RINGS][0:rows, j, :], in_offset=None).then_inc(sent[g % RINGS], 16)

            for g in range(GROUPS - 2):
                scatter(g)

            def carry_waits(n):
                pool.wait_ge(S["carried"], n)
                pool.tensor_tensor(fence[:], fence[:], fence[:], ALU.add).then_inc(S["carried"], 1)

            def send_y(s, q, n):
                pool.wait_ge(S["y_ready"], 2 * s + 2)
                if later(s, 1):
                    pool.wait_ge(S["y_sent"], 32 * s)
                carry_waits(n)
                for h in range(2):
                    pool.indirect_dma_start(out=out[:, :], out_offset=bass.IndirectOffsetOnAxis(y_row[:, q, h:h + 1], 0),
                                            in_=ybuf[:, q % 2, h, :], in_offset=None,
                                            compute_op=ALU.add).then_inc(S["y_sent"], 16)

            def low_weights(s, b, n):
                pool.wait_ge(S["wcur_high"], s + 1)
                carry_waits(n)
                e = pool.value_load(slot_ei[0:1, bass.ds(s, 1)], min_val=0, max_val=E - 1)
                pool.tensor_tensor(w1cur[:, b, 1, H:EW], w1r[:, bass.ds(e * EW + H, H)], w1cur[:, b, 0, H:EW].bitcast(F32),
                                   ALU.subtract).then_inc(S["wcur_low1"], 1)

            pool.wait_ge(S["w1_in"], 16 * KD)
            pool.wait_ge(S["early_table"], 1)
            low_weights(0, 0, 1)
            low_weights(1, 1, 2)
            scatter(GROUPS - 2, 0, 4)
            low_weights(2, 0, 3)
            low_weights(3, 1, 4)
            scatter(GROUPS - 2, 4, GROUP)
            for t in LAST_STORES:
                q, count = store_of(t)
                pool.wait_ge(x1_kept[q], count)
            pool.wait_ge(S["rows_zeroed"], 16)
            for s in range(8):
                send_y(s, s % 4, 2 * s + 5)
                low_weights(s + 4, s % 2, 2 * s + 6)
                if s < GROUP:
                    scatter(GROUPS - 1, s, s + 1)
            with pool.Fori(2, SLOT_TILES // 4 - 1) as i:
                for q in range(4):
                    send_y(4 * i + q, q, 8 * i + 2 * q + 5)
                    low_weights(4 * i + q + 4, q % 2, 8 * i + 2 * q + 6)
            for q in range(4):
                send_y(SLOT_TILES - 4 + q, q, 2 * SLOT_TILES - 3 + q)

        @block.scalar
        def _(act):
            with act.Fori(0, E // 2) as i:
                for b in range(2):
                    act.wait_ge(stage_w2[b], 16 * i + 16)
                    act.copy(w2h[:, bass.ds((2 * i + b) * EW, EW)], stage[b]).then_inc(S["w2_high"], 1)
            act.wait_ge(S["small_in"], 32)
            act.wait_ge(S["gnn_in"], 16 * GNN_LOADS)
            for k in range(KD):
                act.activation(wr_g[:, k, :], wr_raw[:, k, :], ACT.Copy, scale=gb[:, 0, k:k + 1]).then_inc(S["wrg_ready"], 1)
            act.wait_ge(S["mix_ps"], 2)
            act.copy(mix, bank[2][0:5, 0:D]).then_inc(S["mix_copied"], 1)
            act.copy(br_bc[:], bank[3][:, 0:E]).then_inc(S["mix_copied"], 1)
            act.wait_ge(S["sqrt_in"], 1)
            act.activation(fw[:, 6, :], fw[:, 9, :], ACT.Sqrt).then_inc(S["sqrt_out"], 1)

            for slot in range(LAST_SLOT):
                if slot < TILES:
                    t = slot
                    act.wait_ge(S["hid_ps"], t + 1)
                    if t >= 2:
                        act.wait_ge(S["gnn_ps"], t - 1)
                    act.activation(g_t[:, t % 2, :, :], bank[4 + t % 2][:, 0:KD * P].rearrange("p (k n) -> p k n", k=KD),
                                   ACT.Relu).then_inc(S["hid_ready"], 1)
                g, rest = divmod(slot - (GROUP + 1), GROUP)
                if rest == 0 and 0 <= g < GROUPS:
                    act.wait_ge(S["var_ready"], g + 1)
                    act.activation(rt[:, 1, :], rt[:, 0, :], ACT.Sqrt).then_inc(S["std_ready"], 1)
                for t in u_tiles(slot):
                    g, j = divmod(t, GROUP)
                    act.wait_ge(S["norm_ready"], g + 1)
                    q, count = store_of(t)
                    act.wait_ge(x1_kept[q], count)
                    act.activation(ring[g % RINGS][:, j, 0:D], ring[g % RINGS][:, j, 0:D], ACT.Identity,
                                   bias=nmean[:, g % RINGS, j:j + 1], scale=rstd[:, g % RINGS, j:j + 1]).then_inc(S["u_ready"], 1)
                for t in u_tiles(slot - 1):
                    act.wait_ge(S["ut_ps"], t + 1)
                    if t >= 2:
                        act.wait_ge(S["logit_ps"], t - 1)
                    act.copy(u_t[:, t % 2, :, :],
                             bank[2 + t % 2][:, 0:KD * P].rearrange("p (k n) -> p k n", k=KD)).then_inc(S["ut_ready"], 1)

            def affine(s, b):
                act.wait_ge(S["xt_ps"], s + 1)
                if later(s, 2):
                    act.wait_ge(S["xt_ready"], s - 1)
                for k in range(KD):
                    act.activation(xn[:, b, k, :], bank[b][:, k * TILE:(k + 1) * TILE], ACT.Identity,
                                   bias=gb[:, 1, k:k + 1], scale=gb[:, 0, k:k + 1]).then_inc(S["xn_ready"], 1)

            def tanh(s, b):
                act.wait_ge(S["lead_ready"], s + 1)
                if later(s, 2):
                    act.wait_ge(S["weight_ready"], s - 1)
                act.activation(half_tanh[:, b, :], lead[:, b, 1, :], ACT.Tanh, scale=0.5).then_inc(S["tanh_ready"], 1)

            def high_weights(s, b, e):
                if later(s, 2):
                    act.wait_ge(S["h_ps"], KH * (s - 1))
                act.copy(w1cur[:, b, 0, :], w1r[:, bass.ds(e * EW, EW)]).then_inc(S["wcur_high"], 1)

            def gelu(s, b, m):
                act.wait_ge(S["h_ps"], KH * s + m // 2 * 2 + 2)
                if later(s, 2):
                    act.wait_ge(S["htl_ready"], 2 * (s - 1))
                act.activation(hbuf[:, b, m, :], bank[2 + 2 * b + m // 2][:, (m % 2) * TILE:(m % 2 + 1) * TILE], ACT.Gelu,
                               bias=b1cur[:, b, m:m + 1]).then_inc(S["h_ready"], 1)

            def high_h(s, b):
                act.wait_ge(S["h_ready"], KH * s + 2)
                if later(s, 2):
                    act.wait_ge(S["y_ps"], 2 * (s - 1))
                act.copy(hth[:, b, 0:2, :], hbuf[:, b, 0:2, :]).then_inc(S["hth_first"], 1)

            def scale_y(s, q):
                act.wait_ge(S["yb_ready"], s + 1)
                for h in range(2):
                    act.activation(ybuf[:, q % 2, h, :], ybuf[:, q % 2, h, :], ACT.Copy,
                                   scale=weight[:, q, h:h + 1]).then_inc(S["y_ready"], 1)

            def expert_step(s, q, to_come=4):
                b = q % 2
                gelu(s, b, 0)
                gelu(s, b, 1)
                high_h(s, b)
                gelu(s, b, 2)
                if to_come > 1 and later(s, 1):
                    affine(s + 1, 1 - b)
                gelu(s, b, 3)
                if to_come > 1 and later(s, 1):
                    tanh(s + 1, 1 - b)
                if later(s, 2):
                    scale_y(s - 2, (q - 2) % 4)
                if to_come > 2:
                    e = act.value_load(slot_ei[0:1, bass.ds(s + 2, 1)], min_val=0, max_val=E - 1)
                    high_weights(s + 2, b, e)

            act.wait_ge(S["early_table"], 1)
            act.wait_ge(S["w1_in"], 16 * KD)
            for s in range(2):
                e = act.value_load(slot_ei[0:1, s:s + 1], min_val=0, max_val=E - 1)
                high_weights(s, s, e)
            for s in range(2):
                tanh(s, s)
                affine(s, s)
            for q in range(4):
                expert_step(q, q)
            with act.Fori(0, (SLOT_TILES - 8) // 8) as i:
                for q in range(8):
                    expert_step(8 * i + 4 + q, q)
            for q in range(4):
                expert_step(SLOT_TILES - 4 + q, q, to_come=4 - q)
            scale_y(SLOT_TILES - 2, 2)
            scale_y(SLOT_TILES - 1, 3)

        @block.vector
        def _(dve):
            steps = [0]

            def then(ins):
                steps[0] += 1
                ins.then_inc(S["dve_step"], 1)
                dve.wait_ge(S["dve_step"], steps[0])

            dve.wait_ge(S["dst_in"], 16)
            dve.tensor_scalar(hi_i[0:EP, :], dst_i[0:EP, :], 6, None, ALU.logical_shift_right).then_inc(S["dve_step"], 1)
            dve.tensor_scalar(lo_i[0:EP, :], dst_i[0:EP, :], LO - 1, None, ALU.bitwise_and).then_inc(S["dve_step"], 1)
            steps[0] += 2
            dve.wait_ge(S["dve_step"], 2)
            dve.tensor_copy(dst_hi[0:EP, :], hi_i[0:EP, :]).then_inc(S["dve_step"], 1)
            dve.tensor_copy(dst_lo[0:EP, :], lo_i[0:EP, :]).then_inc(S["dve_step"], 1)
            steps[0] += 2
            dve.wait_ge(S["dve_step"], 4)
            dve.wait_ge(S["numbers"], 2)

            def onehots(c, b):
                cols = bass.ds(c * OH_TILES, OH_TILES)
                dve.tensor_tensor(oh_hi[0:EP, b, :, :], dst_hi[0:EP, cols].unsqueeze(1).to_broadcast([EP, HI, OH_TILES]),
                                  num_hi[0:EP, :, :], ALU.is_equal)
                dve.tensor_tensor(oh_lo[0:EP, b, :, :], dst_lo[0:EP, cols].unsqueeze(1).to_broadcast([EP, LO, OH_TILES]),
                                  num_lo[0:EP, :, :], ALU.is_equal).then_inc(S["onehot"], 1)

            for b in range(4):
                onehots(b, b)
            with dve.Fori(1, CHUNKS // 4) as i:
                for b in range(4):
                    dve.wait_ge(S["onehot_used"], 4 * i + b - 3)
                    onehots(4 * i + b, b)
            for c in range(CHUNKS - 2, CHUNKS):
                dve.wait_ge(S["onehot_used"], c - 3)
                onehots(c, c % 4)

            dve.wait_ge(S["degree"], 1)
            dve.wait_ge(S["gnn_in"], 16 * GNN_LOADS)
            then(dve.tensor_scalar(fw[:, 0, :], bank[0][0:HI, 0:LO], 1.0 / (N - 1), None, ALU.mult))
            dve.tensor_scalar(fw[:, 9, :], fw[:, 0, :], 1e-30, None, ALU.max).then_inc(S["sqrt_in"], 1)
            dve.tensor_scalar(fw[:, 7, :], fw[:, 0, :], 1e-8, None, ALU.add)
            then(dve.tensor_tensor(fw[:, 5, :], fw[:, 0, :], noise, ALU.mult))
            dve.scalar_tensor_tensor(fw[:, 1, :], fw[:, 5, :], 0.1, fw[:, 0, :], ALU.mult, ALU.add)
            dve.memset(fw[:, 4, :], 1.0)
            then(dve.reciprocal(fw[:, 2, :], fw[:, 7, :]))
            dve.wait_ge(S["sqrt_out"], 1)
            dve.reciprocal(fw[:, 10, :], fw[:, 6, :])
            then(dve.tensor_tensor(fw[:, 8, :], fw[:, 6, :], fw[:, 6, :], ALU.mult))
            then(dve.tensor_tensor(fw[:, 8, :], fw[:, 0, :], fw[:, 8, :], ALU.subtract))
            then(dve.tensor_tensor(fw[:, 8, :], fw[:, 8, :], fw[:, 10, :], ALU.mult))
            then(dve.scalar_tensor_tensor(fw[:, 3, :], fw[:, 8, :], 0.5, fw[:, 6, :], ALU.mult, ALU.add))
            dve.wait_ge(S["prep_done"], 1)
            then(dve.tensor_copy(fparts[:, 0, :, :], fw[:, 0:5, :]))
            then(dve.tensor_tensor(frest, fw[:, 0:5, :], fparts[:, 0, :, :], ALU.subtract))
            then(dve.tensor_copy(fparts[:, 1, :, :], frest))
            then(dve.tensor_tensor(frest, frest, fparts[:, 1, :, :], ALU.subtract))
            dve.tensor_copy(fparts[:, 2, :, :], frest).then_inc(S["feats_ready"], 1)

            def norm(g):
                if g:
                    dve.wait_ge(S["norm_ready"], g)
                dve.wait_ge(S["stats_ready"], GROUP * (g + 1))
                for j in range(GROUP):
                    last = dve.bn_aggr(mv[:, j, :], stats[:, g % 2, j, :])
                then(last)
                dve.tensor_scalar(rt[:, 0, :], mv[:, :, 1], 1.0 + LN_EPS, LN_EPS * LN_EPS, ALU.mult, ALU.add).then_inc(S["var_ready"], 1)

            def refine(g):
                dve.wait_ge(S["std_ready"], g + 1)
                then(dve.reciprocal(rt[:, 2, :], rt[:, 1, :]))
                then(dve.tensor_tensor(rt[:, 3, :], rt[:, 2, :], rt[:, 2, :], ALU.mult))
                then(dve.tensor_tensor(rt[:, 3, :], rt[:, 3, :], rt[:, 0, :], ALU.mult))
                then(dve.tensor_scalar(rt[:, 3, :], rt[:, 3, :], -0.5, 1.5, ALU.mult, ALU.add))
                then(dve.tensor_tensor(rstd[:, g % RINGS, :], rt[:, 3, :], rt[:, 2, :], ALU.mult))
                dve.scalar_tensor_tensor(nmean[:, g % RINGS, :], mv[:, :, 0], -1.0, rstd[:, g % RINGS, :],
                                         ALU.mult, ALU.mult).then_inc(S["norm_ready"], 1)

            wide = [P, GROUP, E]
            rev_b = rev[:, :].unsqueeze(1).to_broadcast(wide)

            def best_of(of, best, rank, onehot):
                then(dve.tensor_reduce(best[:], of[:], AX_X, ALU.max))
                then(dve.tensor_tensor(eqm[:], of[:], best[:, :].unsqueeze(2).to_broadcast(wide), ALU.is_equal))
                then(dve.tensor_tensor(eqm[:], eqm[:], rev_b, ALU.mult))
                then(dve.tensor_reduce(rank[:], eqm[:], AX_X, ALU.max))
                then(dve.tensor_tensor(onehot[:], rev_b, rank[:, :].unsqueeze(2).to_broadcast(wide), ALU.is_equal))

            def route_first(g):
                dve.wait_ge(S["logit_ps"], GROUP * (g + 1))
                dve.tensor_tensor(lg[:], bank[0][:, 0:GROUP * E].rearrange("p (j e) -> p j e", e=E),
                                  br_bc[:, :].unsqueeze(1).to_broadcast(wide), ALU.add).then_inc(S["logits_read"], 1)
                dve.wait_ge(S["logits_read"], g + 1)
                best_of(lg, m1, r1, oh1)

            def route_second(g):
                then(dve.scalar_tensor_tensor(lg2[:], oh1[:], -3e38, lg[:], ALU.mult, ALU.add))
                best_of(lg2, m2, r2, oh2)

            def route_mask(g):
                if g == GROUPS - 1:
                    dve.tensor_scalar(oh1[:, GROUP - 1, :], oh1[:, GROUP - 1, :], valid[:], None, ALU.mult)
                    then(dve.tensor_scalar(oh2[:, GROUP - 1, :], oh2[:, GROUP - 1, :], valid[:], None, ALU.mult))
                dve.tensor_tensor(both[:, GROUP:2 * GROUP, :], oh1[:], oh2[:], ALU.add).then_inc(S["mask_ready"], 1)
                r = g % RINGS
                dve.tensor_copy(ring[r][:, :, D], node_id[:, g * GROUP:(g + 1) * GROUP])
                dve.tensor_scalar(ring[r][:, :, D + 1], r1[:], -1.0, float(E), ALU.mult, ALU.add)
                dve.tensor_tensor(ring[r][:, :, D + 2], m1[:], m2[:], ALU.subtract)

            def route_places(g):
                r = g % RINGS
                dve.wait_ge(S["pos_ps"], g + 1)
                then(dve.tensor_tensor(posE[:], bank[1][:, 0:GROUP * E].rearrange("p (j e) -> p j e", e=E),
                                       fill[:, :].unsqueeze(1).to_broadcast(wide), ALU.add))
                dve.tensor_tensor(oh1[:], oh1[:], posE[:], ALU.mult)
                then(dve.tensor_tensor(oh2[:], oh2[:], posE[:], ALU.mult))
                dve.tensor_tensor(fill[:], fill[:], bank[1][:, GROUP * E:(GROUP + 1) * E], ALU.add)
                dve.tensor_reduce(dest[:, r, 0, :], oh1[:], AX_X, ALU.add)
                dve.tensor_reduce(dest[:, r, 1, :], oh2[:], AX_X, ALU.add).then_inc(S["dest_ready"], 1)

            def table_counts(fill, late):
                then(dve.tensor_tensor(jump[:], fill[:], regions[:], ALU.subtract))
                then(dve.tensor_scalar(cnt_i[:], jump[:], float(TILE - 1) if late else 0.0, None, ALU.add))
                dve.memset(cum[:], 0.0)
                then(dve.tensor_scalar(ntile_i[:], cnt_i[:], 8, None, ALU.logical_shift_right))
                then(dve.tensor_copy(ntile[:], ntile_i[:]))
                if late:
                    then(dve.tensor_tensor(ntile[:], ntile[:], early[:, 0:E], ALU.subtract))
                then(dve.tensor_copy(cum[:, 0, 4:4 + E], ntile[:]))

            def table_sums(late):
                for k, d in enumerate((1, 2, 4)):
                    then(dve.tensor_tensor(cum[:, (k + 1) % 2, 4:4 + E], cum[:, k % 2, 4:4 + E],
                                           cum[:, k % 2, 4 - d:4 + E - d], ALU.add))
                then(dve.tensor_scalar(jump[:], ntile[:], -float(TILE), float(REGION), ALU.mult, ALU.add))
                if late:
                    then(dve.tensor_tensor(ntile[:], early[:, 1:E + 1], early[:, 0:E], ALU.subtract))
                    then(dve.scalar_tensor_tensor(jump[:], ntile[:], float(TILE), jump[:], ALU.mult, ALU.add))

            def table_rows(first, end):
                n = end - first
                size = [P, n, E]
                then(dve.tensor_tensor(cmp_a[:, 0:n, :], slot_no[:, 0:n].unsqueeze(2).to_broadcast(size),
                                       cum[:, 1, 4:4 + E].unsqueeze(1).to_broadcast(size), ALU.is_ge))
                dve.tensor_reduce(slot_e[:, first:end], cmp_a[:, 0:n, :], AX_X, ALU.add)
                then(dve.tensor_tensor(cmp_b[:, 0:n, :], cmp_a[:, 0:n, :], jump[:, :].unsqueeze(1).to_broadcast(size), ALU.mult))
                dve.tensor_scalar(slot_ei[:, first:end], slot_e[:, first:end], float(E - 1), None, ALU.min)
                then(dve.tensor_reduce(slot_f[:, 0:n], cmp_b[:, 0:n, :], AX_X, ALU.add))
                then(dve.scalar_tensor_tensor(slot_f[:, 0:n], slot_no[:, 0:n], float(TILE), slot_f[:, 0:n], ALU.mult, ALU.add))
                if first:
                    then(dve.tensor_scalar(start[:], early[:, 0:1], float(TILE), None, ALU.mult))
                    dve.tensor_scalar(slot_row[:, first:end], slot_f[:, 0:n], start[:], float(SPARE_AT), ALU.add,
                                      ALU.min).then_inc(S["late_table"], 1)
                    return
                dve.memset(early[:], 0.0)
                then(dve.tensor_scalar(cum[:, 0, 3:4 + E], cum[:, 1, 3:4 + E], float(end), None, ALU.min))
                then(dve.tensor_tensor(early[:, 0:E], cum[:, 0, 4:4 + E], cum[:, 0, 3:3 + E], ALU.subtract))
                dve.tensor_copy(slot_row[:, first:end], slot_f[:, 0:n]).then_inc(S["early_table"], 1)

            dve.wait_ge(S["prep_done"], 1)
            dve.tensor_scalar(valid[:], node_id[:, 0:1], float(TAIL), None, ALU.is_lt)
            ROUTING = ((ROUTE_SLOT, route_first), (ROUTE_SLOT + 1, route_second), (ROUTE_SLOT + 2, route_mask),
                       (PLACE_SLOT, route_places))
            for slot in range(1, LAST_SLOT + 1):
                if slot <= TILES:
                    t = slot - 1
                    g, j = divmod(t, GROUP)
                    if j == 0:
                        dve.wait_ge(x_in[g % RINGS], 16 if g < RINGS else 32 if g + 1 < GROUPS else 48)
                    dve.wait_ge(S["gnn_ps"], t + 1)
                    xr = ring[g % RINGS][:, j, 0:D]
                    dve.tensor_tensor(xr, xr, bank[6 + t % 2][:, 0:D], ALU.add).then_inc(S["x1_ready"], 1)
                    dve.wait_ge(S["x1_ready"], t + 1)
                    dve.bn_stats(stats[:, g % 2, j, :], xr).then_inc(S["stats_ready"], 1)
                for g in range(GROUPS):
                    if slot == GROUP * g + GROUP:
                        norm(g)
                    if slot == GROUP * g + GROUP + 1:
                        refine(g)
                for g in range(GROUPS):
                    for at, part in ROUTING:
                        if slot == GROUP * g + at:
                            part(g)
                    if g == EARLY_GROUPS - 1 and slot == GROUP * g + PLACE_SLOT:
                        dve.wait_ge(S["dest_ready"], EARLY_GROUPS)
                        then(dve.tensor_copy(early_fill[:], fill[:]))
                    if g == GROUPS - 2 and slot == GROUP * g + PLACE_SLOT:
                        table_counts(early_fill, late=False)
                        table_sums(late=False)
                        table_rows(0, EARLY)

            dve.wait_ge(S["dest_ready"], GROUPS)
            dve.tensor_copy(pad_at[:], fill[:]).then_inc(S["fill_ready"], 1)

            def leads(s, b, in_count):
                dve.wait_ge(xg_in[b], in_count)
                if later(s, 2):
                    dve.wait_ge(S["tanh_ready"], s - 1)
                e1, gap = xg[:, b, :, D + 1], xg[:, b, :, D + 2]
                dve.scalar_tensor_tensor(lead[:, b, 0, :], e1, slot_e[:, bass.ds(s, 1)], gap,
                                         ALU.is_equal, ALU.mult).then_inc(S["lead_step"], 1)
                dve.wait_ge(S["lead_step"], s + 1)
                dve.scalar_tensor_tensor(lead[:, b, 1, :], lead[:, b, 0, :], 2.0, gap, ALU.mult, ALU.subtract).then_inc(S["lead_ready"], 1)

            def low_weights(s, b, e):
                if later(s, 2):
                    dve.wait_ge(S["h_ready"], KH * (s - 1))
                dve.tensor_copy(b1cur[:, b, :], b1t[:, bass.ds(e * KH, KH)])
                dve.wait_ge(S["wcur_high"], s + 1)
                dve.tensor_tensor(w1cur[:, b, 1, 0:H], w1r[:, bass.ds(e * EW, H)], w1cur[:, b, 0, 0:H].bitcast(F32),
                                  ALU.subtract).then_inc(S["wcur_low0"], 1)

            def split_x(s, b):
                dve.wait_ge(S["xn_ready"], KD * s + KD)
                if later(s, 2):
                    dve.wait_ge(S["h_ps"], KH * (s - 1))
                dve.tensor_copy(xth[:, b, :, :], xn[:, b, :, :]).then_inc(S["xth_ready"], 1)
                dve.wait_ge(S["xth_ready"], s + 1)
                dve.tensor_tensor(xtl[:, b, :, :], xn[:, b, :, :], xth[:, b, :, :].bitcast(F32),
                                  ALU.subtract).then_inc(S["xt_ready"], 1)

            def split_h(s, b, half):
                m = slice(2 * half, 2 * half + 2)
                if half:
                    dve.wait_ge(S["h_ready"], KH * s + KH)
                    if later(s, 2):
                        dve.wait_ge(S["y_ps"], 2 * (s - 1))
                    dve.tensor_copy(hth[:, b, m, :], hbuf[:, b, m, :]).then_inc(S["hth_second"], 1)
                dve.wait_ge(S["hth_second" if half else "hth_first"], s + 1)
                dve.tensor_tensor(htl[:, b, m, :], hbuf[:, b, m, :], hth[:, b, m, :].bitcast(F32),
                                  ALU.subtract).then_inc(S["htl_ready"], 1)

            def softmax(s, q):
                if later(s, 4):
                    dve.wait_ge(S["y_sent"], 32 * (s - 3))
                dve.tensor_copy(y_row[:, q, :], xg[:, q % 2, :, D])
                dve.wait_ge(S["tanh_ready"], s + 1)
                if later(s, 4):
                    dve.wait_ge(S["y_ready"], 2 * (s - 3))
                dve.tensor_scalar(weight[:, q, :], half_tanh[:, q % 2, :], 0.5, 0.5, ALU.mult, ALU.add).then_inc(S["weight_ready"], 1)

            def bias_y(s, q, e):
                dve.wait_ge(S["y_ps"], 2 * s + 2)
                dve.wait_ge(S["weight_ready"], s + 1)
                if later(s, 2):
                    dve.wait_ge(S["y_sent"], 32 * (s - 1))
                b = q % 2
                dve.tensor_tensor(ybuf[:, b, :, :], bank[6 + b][:, :].rearrange("p (h d) -> p h d", h=2),
                                  b2_bc[:, bass.ds(e * D, D)].unsqueeze(1).to_broadcast([P, 2, D]),
                                  ALU.add).then_inc(S["yb_ready"], 1)

            def expert_step(s, q, next_in, experts, last=False):
                b = q % 2
                if later(s, 2):
                    e = experts[q - 2] if q - 2 in experts else \
                        dve.value_load(slot_ei[0:1, bass.ds(s - 2, 1)], min_val=0, max_val=E - 1)
                    bias_y(s - 2, (q - 2) % 4, e)
                last = last or not later(s, 1)
                if not last:
                    e = experts[q + 1] = dve.value_load(slot_ei[0:1, bass.ds(s + 1, 1)], min_val=0, max_val=E - 1)
                    leads(s + 1, 1 - b, next_in)
                    low_weights(s + 1, 1 - b, e)
                split_h(s, b, 0)
                if not last:
                    split_x(s + 1, 1 - b)
                split_h(s, b, 1)
                if not last:
                    softmax(s + 1, (q + 1) % 4)

            dve.wait_ge(S["w1_in"], 16 * KD)
            dve.wait_ge(S["b1_in"], 16 * KH)
            dve.wait_ge(S["early_table"], 1)
            e = dve.value_load(slot_ei[0:1, 0:1], min_val=0, max_val=E - 1)
            low_weights(0, 0, e)
            leads(0, 0, 16)
            softmax(0, 0)
            split_x(0, 0)
            leads(1, 1, 16)
            e = dve.value_load(slot_ei[0:1, 1:2], min_val=0, max_val=E - 1)
            low_weights(1, 1, e)
            softmax(1, 1)
            split_x(1, 1)
            dve.wait_ge(S["b2_in"], 16)
            experts = {}
            table_counts(fill, late=True)
            table_sums(late=True)
            for q in (0, 1):
                expert_step(q, q, 16 * ((q + 1) // 2 + 1), experts)
            table_rows(EARLY, SLOT_TILES)
            for q in (2, 3):
                expert_step(q, q, 16 * ((q + 1) // 2 + 1), experts)
            with dve.Fori(0, (SLOT_TILES - 8) // 8) as i:
                experts = {}
                for q in range(8):
                    expert_step(8 * i + 4 + q, q, 64 * i + 32 + 16 * ((q + 1) // 2 + 1), experts)
            experts = {}
            for q in range(4):
                s = SLOT_TILES - 4 + q
                expert_step(s, q, 16 * ((s + 1) // 2 + 1), experts, last=q == 3)
            for q in (2, 3):
                bias_y(SLOT_TILES - 4 + q, q, experts[q])

        @block.tensor
        def _(pe):
            pe.wait_ge(S["zeroed"], 1)
            zero_b = zeros.bitcast(BF16)
            pe.matmul(bank[0][0:HI, 0:LO], zero_b[0:EP, 0:HI], zero_b[0:EP, 0:LO], start=True, stop=False)

            def count(c, b):
                pe.wait_ge(S["onehot"], c + 1)
                for t in range(OH_TILES):
                    mm = pe.matmul(bank[0][0:HI, 0:LO], oh_hi[0:EP, b, :, t], oh_lo[0:EP, b, :, t], start=False, stop=False)
                mm.then_inc(S["onehot_used"], 1)

            with pe.Fori(0, 4) as i:
                for b in range(4):
                    count(4 * i + b, b)
            pe.wait_ge(S["gnn_in"], 16 * GNN_LOADS)
            for k in range(KD):
                mm = pe.matmul(bank[2][0:5, 0:D], vec_w[:, k, :], w1g[:, k, :], start=(k == 0), stop=(k == KD - 1))
            mm.then_inc(S["mix_ps"], 1)
            pe.wait_ge(S["beta_bc_ready"], KD)
            for k in range(KD):
                mm = pe.matmul(bank[3][:, 0:E], beta_bc[:, k, :], wr_raw[:, k, :], start=(k == 0), stop=(k == KD - 1))
            mm.then_inc(S["mix_ps"], 1)
            with pe.Fori(4, CHUNKS // 4) as i:
                for b in range(4):
                    count(4 * i + b, b)
            for c in range(CHUNKS - 2, CHUNKS):
                count(c, c % 4)
            pe.matmul(bank[0][0:HI, 0:LO], zero_b[0:EP, 0:HI], zero_b[0:EP, 0:LO], start=False, stop=True).then_inc(S["degree"], 1)

            def hidden(t):
                g, j = divmod(t, GROUP)
                if j == 0:
                    pe.wait_ge(feat_in[g % 2], 48 * (g // 2 + 1))
                if t >= 2:
                    pe.wait_ge(S["hid_ready"], t - 1)
                for k in range(KD):
                    mm = pe.matmul(bank[4 + t % 2][:, k * P:(k + 1) * P], mix_rows[:, k * P:(k + 1) * P],
                                   feat[:, g % 2, j * P:(j + 1) * P], start=True, stop=True)
                mm.then_inc(S["hid_ps"], 1)

            def gnn_out(t):
                pe.wait_ge(S["hid_ready"], t + 1)
                if t >= 2:
                    pe.wait_ge(S["x1_ready"], t - 1)
                o = bank[6 + t % 2][:, 0:D]
                pe.matmul(o, three[:, :], b2g, start=True, stop=False)
                for k in range(KD):
                    mm = pe.matmul(o, g_t[:, t % 2, k, :], w2g[:, k, :], start=False, stop=(k == KD - 1))
                mm.then_inc(S["gnn_ps"], 1)

            def turn_u(t):
                g, j = divmod(t, GROUP)
                pe.wait_ge(S["u_ready"], t + 1)
                if t >= 2:
                    pe.wait_ge(S["ut_ready"], t - 1)
                for k in range(KD):
                    mm = pe.transpose(bank[2 + t % 2][:, k * P:(k + 1) * P], ring[g % RINGS][:, j, k * P:(k + 1) * P], ident[:, :])
                mm.then_inc(S["ut_ps"], 1)

            def logits(t):
                g, j = divmod(t, GROUP)
                pe.wait_ge(S["ut_ready"], t + 1)
                if j == 0 and g:
                    pe.wait_ge(S["logits_read"], g)
                for k in range(KD):
                    mm = pe.matmul(bank[0][:, j * E:(j + 1) * E], u_t[:, t % 2, k, :], wr_g[:, k, :],
                                   start=(k == 0), stop=(k == KD - 1))
                mm.then_inc(S["logit_ps"], 1)

            def places(g):
                pe.wait_ge(S["mask_ready"], g + 1)
                m = both[:, :, :].rearrange("p j e -> p (j e)")
                for d in range(GROUP + 1):
                    mm = pe.matmul(bank[1][:, 0:(GROUP + 1) * E], (ones if d else below)[:, :],
                                   m[:, (GROUP - d) * E:(2 * GROUP + 1 - d) * E], start=(d == 0), stop=(d == GROUP))
                mm.then_inc(S["pos_ps"], 1)

            pe.wait_ge(S["prep_done"], 1)
            pe.wait_ge(S["mix_placed"], 6 * 16)
            pe.wait_ge(S["wrg_ready"], KD)
            for slot in range(LAST_SLOT + 1):
                if slot < TILES:
                    hidden(slot)
                if 1 <= slot <= TILES:
                    gnn_out(slot - 1)
                for t in u_tiles(slot - 1):
                    turn_u(t)
                for t in u_tiles(slot - 2):
                    logits(t)
                g, rest = divmod(slot - PLACE_SLOT, GROUP)
                if g >= 0 and rest == 0:
                    places(g)

            def turn_x(s, b, in_count):
                pe.wait_ge(xg_in[b], in_count)
                if later(s, 2):
                    pe.wait_ge(S["xt_ready"], s - 1)
                for h in range(2):
                    for k in range(KD):
                        mm = pe.transpose(bank[b][:, k * TILE + h * P:k * TILE + (h + 1) * P],
                                          xg[:, b, h, k * P:(k + 1) * P], ident[:, :])
                mm.then_inc(S["xt_ps"], 1)

            def layer1(s, b):
                pe.wait_ge(S["xt_ready"], s + 1)
                pe.wait_ge(S["wcur_low0"], s + 1)
                pe.wait_ge(S["wcur_low1"], s + 1)
                if later(s, 2):
                    pe.wait_ge(S["h_ready"], KH * (s - 1))
                for m in range(KH):
                    o = bank[2 + 2 * b + m // 2][:, (m % 2) * TILE:(m % 2 + 1) * TILE]
                    for k in range(KD):
                        cols = slice(k * H + m * P, k * H + (m + 1) * P)
                        pe.matmul(o, w1cur[:, b, 0, cols], xth[:, b, k, :], start=(k == 0), stop=False)
                        pe.matmul(o, w1cur[:, b, 0, cols], xtl[:, b, k, :], start=False, stop=False)
                        mm = pe.matmul(o, w1cur[:, b, 1, cols], xth[:, b, k, :], start=False, stop=(k == KD - 1))
                    mm.then_inc(S["h_ps"], 1)

            def layer2(s, b):
                e = pe.value_load(slot_ei[0:1, bass.ds(s, 1)], min_val=0, max_val=E - 1)
                pe.wait_ge(S["htl_ready"], 2 * s + 2)
                if later(s, 2):
                    pe.wait_ge(S["yb_ready"], s - 1)
                for h in range(2):
                    o = bank[6 + b][:, h * D:(h + 1) * D]
                    tok = slice(h * P, (h + 1) * P)
                    for k in range(KH):
                        high = w2h[:, bass.ds(e * EW + k * D, D)]
                        low = w2l[:, bass.ds(e * EW + k * D, D)]
                        pe.matmul(o, hth[:, b, k, tok], high, start=(k == 0), stop=False)
                        pe.matmul(o, hth[:, b, k, tok], low, start=False, stop=False)
                        mm = pe.matmul(o, htl[:, b, k, tok], high, start=False, stop=(k == KH - 1))
                    mm.then_inc(S["y_ps"], 1)

            def expert_step(s, q, next_in, last=False):
                b = q % 2
                layer1(s, b)
                if not last and later(s, 1):
                    turn_x(s + 1, 1 - b, next_in)
                if later(s, 1):
                    layer2(s - 1, 1 - b)

            pe.wait_ge(S["dest_ready"], GROUPS)
            turn_x(0, 0, 16)
            turn_x(1, 1, 16)
            for q in range(2):
                expert_step(q, q, 16 * ((q + 1) // 2 + 1))
            with pe.Fori(1, SLOT_TILES // 2 - 1) as i:
                for q in range(2):
                    expert_step(2 * i + q, q, 16 * i + 16 * ((q + 1) // 2 + 1))
            for q in range(2):
                s = SLOT_TILES - 2 + q
                expert_step(s, q, 16 * ((s + 1) // 2 + 1), last=q == 1)
            layer2(SLOT_TILES - 1, 1)


_INS = ["x", "dst", "node_vec", "L0_gnn_W_deg", "L0_gnn_b_deg", "L0_gnn_W_bet", "L0_gnn_b_bet", "L0_gnn_W_clo",
        "L0_gnn_b_clo", "L0_gnn_W_eig", "L0_gnn_b_eig", "L0_gnn_W1", "L0_gnn_b1", "L0_gnn_W2", "L0_gnn_b2",
        "L0_ffn_gamma", "L0_ffn_beta", "L0_ffn_Wr", "L0_ffn_br", "L0_ffn_W1", "L0_ffn_b1", "L0_ffn_W2", "L0_ffn_b2"]


def kernel(**inputs):
    import numpy as _np
    import concourse.bacc as _bacc
    from concourse import mybir as _mybir
    from concourse.bass_utils import run_bass_kernel_spmd as _run

    nc = _bacc.Bacc("TRN2", target_bir_lowering=False, num_devices=1)
    arrays, args = {}, []
    for name in _INS:
        a = _np.ascontiguousarray(inputs[name])
        arrays[f"in_{name}_dram"] = a
        args.append(nc.dram_tensor(f"in_{name}_dram", a.shape, _mybir.dt.from_np(a.dtype), kind="ExternalInput").ap())
    n, d = inputs["x"].shape
    args.append(nc.dram_tensor("out_0_dram", (n + TILE, d), _mybir.dt.float32, kind="ExternalOutput").ap())
    gnn_ffn_kernel(nc, *args)
    r = _run(nc, [arrays], core_ids=[0])
    return r.results[0]["out_0_dram"][:n]
```
